# Optimizing a Trainium2 kernel written in Bass

```python
import numpy as np
import jax
import jax.numpy as jnp

def _softmax(x, axis=-1):
    return jax.nn.softmax(x, axis=axis)

def _gelu(x):
    return jax.nn.gelu(x, approximate=True)

def _silu(x):
    return jax.nn.silu(x)

def _sigmoid(x):
    return jax.nn.sigmoid(x)

def _layernorm(x, axis=-1, eps=1e-05):
    m = jnp.mean(x, axis=axis, keepdims=True)
    v = jnp.var(x, axis=axis, keepdims=True)
    return (x - m) / jnp.sqrt(v + eps)

def _scatter_add(tgt, idx, src, axis=0):
    return tgt.at[idx].add(src)

def _segment_sum(src, seg, n):
    return jax.ops.segment_sum(src, seg, n)
kernel_name = 'mk_cond_seq_d2_seqx_r4_622d43'

def setup_inputs(seed: int=0):
    np.random.seed(seed)
    _w = jnp.asarray

    def _rec_inputs():
        import jax
        import jax.numpy as jnp
        _rk = jax.random.key(seed)
        x = 0.5 + 0.2887 * jax.random.normal(jax.random.fold_in(_rk, 1), (8, 256, 512), jnp.float32)
        _lenS = 256 - jax.random.randint(jax.random.fold_in(_rk, 7), (8,), 0, max(1, 256 // 4) + 1, jnp.int32)
        _lenS2 = 256 - jax.random.randint(jax.random.fold_in(_rk, 8), (8,), 0, max(1, 256 // 4) + 1, jnp.int32)
        itok_B_17_1546 = jax.random.randint(jax.random.fold_in(_rk, 12), (8,), 17, 1547, jnp.int32)
        itok_B_1_2 = jax.random.randint(jax.random.fold_in(_rk, 13), (8,), 1, 3, jnp.int32)
        return (x, itok_B_17_1546, itok_B_1_2, _lenS)
    x, itok_B_17_1546, itok_B_1_2, _lenS = _rec_inputs()

    def _L0_cond_setup():
        import jax, jax.numpy as jnp
        import numpy as np
        B, T, V = (8, 128, 512)
        H = 4 * V
        key = jax.random.key(seed)
        ks = jax.random.split(key, 16)
        s = lambda n: 1.0 / np.sqrt(n)
        inp = {'x': jax.random.uniform(ks[0], (B, T, V), dtype=jnp.float32), 'lens': jax.random.randint(ks[1], (B,), 1, T, dtype=jnp.int64), 'target_codes': jax.random.randint(ks[2], (B,), 0, V, dtype=jnp.int64), 'Wq': jax.random.normal(ks[3], (V, V), jnp.float32) * s(V), 'Wk': jax.random.normal(ks[4], (V, V), jnp.float32) * s(V), 'Wv': jax.random.normal(ks[5], (V, V), jnp.float32) * s(V), 'Wp': jax.random.normal(ks[6], (V, V), jnp.float32) * s(V), 'bp': jnp.zeros((V,), jnp.float32), 'cW1': jax.random.normal(ks[7], (V, H), jnp.float32) * s(V), 'cb1': jnp.zeros((H,), jnp.float32), 'cW2': jax.random.normal(ks[8], (H, V), jnp.float32) * s(H), 'cb2': jnp.zeros((V,), jnp.float32), 'mW1': jax.random.normal(ks[9], (2 * V, H), jnp.float32) * s(2 * V), 'mb1': jnp.zeros((H,), jnp.float32), 'mW2': jax.random.normal(ks[10], (H, V), jnp.float32) * s(H), 'mb2': jnp.zeros((V,), jnp.float32)}
        return inp
    _L0_cond_all = _L0_cond_setup()
    _L0_cond_in = {k: v for k, v in _L0_cond_all.items() if k in ('Wq', 'Wk', 'Wv', 'Wp', 'bp', 'cW1', 'cb1', 'cW2', 'cb2', 'mW1', 'mb1', 'mW2', 'mb2')}
    del _L0_cond_all

    def _L1_cond_setup():
        import jax, jax.numpy as jnp
        import numpy as np
        B, S, H = (8, 512, 512)
        BN = 256
        E = 3
        LN_EPS = 1e-05
        key = jax.random.key(seed)
        ks = jax.random.split(key, 8)
        stream = jax.random.randint(ks[0], (B,), 0, E, dtype=jnp.int32)
        hidden_states = jax.random.normal(ks[1], (B, S, H), dtype=jnp.float32)
        W_down = jax.random.normal(ks[2], (E, H, BN), dtype=jnp.float32) * 0.02
        b_down = jnp.zeros((E, BN), dtype=jnp.float32)
        W_up = jax.random.normal(ks[3], (E, BN, H), dtype=jnp.float32) * 0.02
        b_up = jnp.zeros((E, H), dtype=jnp.float32)
        ln_w = jnp.ones((E, H), dtype=jnp.float32)
        ln_b = jnp.zeros((E, H), dtype=jnp.float32)
        return {'stream': stream, 'hidden_states': hidden_states, 'W_down': W_down, 'b_down': b_down, 'W_up': W_up, 'b_up': b_up, 'ln_w': ln_w, 'ln_b': ln_b}
    _L1_cond_all = _L1_cond_setup()
    _L1_cond_in = {k: v for k, v in _L1_cond_all.items() if k in ('W_down', 'b_down', 'W_up', 'b_up', 'ln_w', 'ln_b')}
    del _L1_cond_all
    return {'x': x, 'itok_B_17_1546': itok_B_17_1546, 'itok_B_1_2': itok_B_1_2, '_lenS': _lenS, 'L0_cond_Wq': _L0_cond_in['Wq'], 'L0_cond_Wk': _L0_cond_in['Wk'], 'L0_cond_Wv': _L0_cond_in['Wv'], 'L0_cond_Wp': _L0_cond_in['Wp'], 'L0_cond_bp': _L0_cond_in['bp'], 'L0_cond_cW1': _L0_cond_in['cW1'], 'L0_cond_cb1': _L0_cond_in['cb1'], 'L0_cond_cW2': _L0_cond_in['cW2'], 'L0_cond_cb2': _L0_cond_in['cb2'], 'L0_cond_mW1': _L0_cond_in['mW1'], 'L0_cond_mb1': _L0_cond_in['mb1'], 'L0_cond_mW2': _L0_cond_in['mW2'], 'L0_cond_mb2': _L0_cond_in['mb2'], 'L1_cond_W_down': _L1_cond_in['W_down'], 'L1_cond_b_down': _L1_cond_in['b_down'], 'L1_cond_W_up': _L1_cond_in['W_up'], 'L1_cond_b_up': _L1_cond_in['b_up'], 'L1_cond_ln_w': _L1_cond_in['ln_w'], 'L1_cond_ln_b': _L1_cond_in['ln_b']}

def reference(x, itok_B_17_1546, itok_B_1_2, _lenS, L0_cond_Wq, L0_cond_Wk, L0_cond_Wv, L0_cond_Wp, L0_cond_bp, L0_cond_cW1, L0_cond_cb1, L0_cond_cW2, L0_cond_cb2, L0_cond_mW1, L0_cond_mb1, L0_cond_mW2, L0_cond_mb2, L1_cond_W_down, L1_cond_b_down, L1_cond_W_up, L1_cond_b_up, L1_cond_ln_w, L1_cond_ln_b):
    import jax
    import jax.numpy as jnp

    def _L0_cond_ref(x, lens, target_codes, Wq, Wk, Wv, Wp, bp, cW1, cb1, cW2, cb2, mW1, mb1, mW2, mb2):
        import jax, jax.numpy as jnp
        import numpy as np
        B, T, V = (8, 128, 512)
        H = 4 * V
        scale = V ** (-0.5)
        q = x @ Wq
        k = x @ Wk
        v = x @ Wv
        attn = jnp.einsum('btd,bTd->btT', q, k) * scale
        attn = jax.nn.softmax(attn, axis=-1)
        attn_out = jnp.einsum('btT,bTd->btd', attn, v) @ Wp + bp
        target_embed = jax.nn.one_hot(target_codes, V, dtype=x.dtype)[:, None, :]
        cms_out = jax.nn.gelu(attn_out @ cW1 + cb1, approximate=False) @ cW2 + cb2
        cms_out = cms_out + target_embed
        concat = jnp.concatenate([attn_out, cms_out], axis=-1)
        modifier = jax.nn.gelu(concat @ mW1 + mb1, approximate=False) @ mW2 + mb2
        out = jnp.clip(x + cms_out + modifier, 0.0, 1.0)
        return out

    def _L1_cond_ref(stream, hidden_states, W_down, b_down, W_up, b_up, ln_w, ln_b):
        import jax, jax.numpy as jnp
        import numpy as np
        B, S, H = (8, 512, 512)
        BN = 256
        E = 3
        LN_EPS = 1e-05
        Wd = W_down[stream]
        bd = b_down[stream]
        Wu = W_up[stream]
        bu = b_up[stream]
        g = ln_w[stream]
        b = ln_b[stream]
        residual = hidden_states
        h = jnp.einsum('bsh,bhk->bsk', hidden_states, Wd) + bd[:, None, :]
        h = jax.nn.gelu(h, approximate=False)
        h = jnp.einsum('bsk,bkh->bsh', h, Wu) + bu[:, None, :]
        h = residual + h
        mean = jnp.mean(h, axis=-1, keepdims=True)
        var = jnp.mean(jnp.square(h - mean), axis=-1, keepdims=True)
        h = (h - mean) * jax.lax.rsqrt(var + LN_EPS)
        return h * g[:, None, :] + b[:, None, :]
    x = _L0_cond_ref(x, _lenS, itok_B_17_1546, L0_cond_Wq, L0_cond_Wk, L0_cond_Wv, L0_cond_Wp, L0_cond_bp, L0_cond_cW1, L0_cond_cb1, L0_cond_cW2, L0_cond_cb2, L0_cond_mW1, L0_cond_mb1, L0_cond_mW2, L0_cond_mb2)
    x = _L1_cond_ref(itok_B_1_2, x, L1_cond_W_down, L1_cond_b_down, L1_cond_W_up, L1_cond_b_up, L1_cond_ln_w, L1_cond_ln_b)
    return x

_drawn_inputs = setup_inputs


def setup_inputs(seed=0):
    import zlib

    import numpy as np

    out = dict(_drawn_inputs(seed))
    spreads = {'L0_cond_bp': (0.0, 0.1),
     'L0_cond_cb1': (0.0, 0.1),
     'L0_cond_cb2': (0.0, 0.1),
     'L0_cond_mb1': (0.0, 0.1),
     'L0_cond_mb2': (0.0, 0.1),
     'L1_cond_b_down': (0.0, 0.1),
     'L1_cond_b_up': (0.0, 0.1),
     'L1_cond_ln_w': (1.0, 0.2),
     'L1_cond_ln_b': (0.0, 0.1)}
    factors = {'L0_cond_Wq': 8.0, 'L0_cond_Wk': 8.0}
    for name, (base, spread) in spreads.items():
        noise = np.random.default_rng([zlib.crc32(name.encode()), seed]).standard_normal(out[name].shape)
        drawn = base * np.exp(spread * noise) if base else spread * noise
        out[name] = jnp.asarray(drawn.astype(out[name].dtype))
    for name, factor in factors.items():
        out[name] = (out[name] * factor).astype(out[name].dtype)
    return out
```

```python
from contextlib import ExitStack

import concourse.bass as bass
from concourse import mybir

F32 = mybir.dt.float32
F32R = mybir.dt.float32r
I32 = mybir.dt.int32
ACT = mybir.ActivationFunctionType
ALU = mybir.AluOpType
AX_X = mybir.AxisListType.X

P = 128
LN_EPS = 1e-5


def build(nc, x, codes, experts, Wq, Wk, Wv, Wp, bp, cW1, cb1, cW2, cb2, mW1, mb1, mW2, mb2,
          W_down, b_down, W_up, b_up, ln_w, ln_b, out):
    B, T, V = x.shape
    H = cW1.shape[1]
    E, _, BN = W_down.shape
    SEQ = 2
    TB = SEQ * T
    NB = B // SEQ
    KT = V // P
    TT = TB // P
    TS = T // P
    MT = BN // P
    NCH = H // P
    CH = 2 * NCH
    UNR = 4
    ITS = NCH // UNR
    SCALE = float(V) ** -0.5
    KIN = (KT, 2 * KT)

    x_rows = x.rearrange("b t v -> (b t) v")
    out_rows = out.rearrange("b t v -> (b t) v")
    mlp_w1 = (cW1.rearrange("(k p) n -> p k n", p=P), mW1.rearrange("(k p) n -> p k n", p=P))
    mlp_w2 = (cW2, mW2)
    square = [w.rearrange("(k p) n -> p k n", p=P) for w in (Wq, Wk, Wv, Wp)]
    down_v = W_down.rearrange("e (k p) n -> p (e k) n", p=P)
    up_v = W_up.rearrange("e (k p) n -> p (e k) n", p=P)
    bdown_v = b_down.rearrange("e (m p) -> (e m) p", p=P)
    row_of = lambda a: a.rearrange("(o b) -> o b", o=1)
    ln_v = (b_up, ln_w, ln_b)
    proj_hi = nc.dram_tensor("proj_hi", (P, 2, KT * V), F32, kind="Internal").ap()
    proj_lo = nc.dram_tensor("proj_lo", (P, 2, KT * V), F32, kind="Internal").ap()

    BIAS = ((bp, V), (cb1, H), (cb2, V), (mb1, H), (mb2, V))
    at, offs = 0, []
    for _, n in BIAS:
        offs.append(at)
        at += n // P
    NROW = at
    BP, CB1, CB2, MB1, MB2 = offs
    MLP_B = (CB1, MB1)

    with ExitStack() as ctx:
        sb = lambda name, shape, dt=F32: ctx.enter_context(nc.sbuf_tensor(name, shape, dt))
        sem = lambda name: ctx.enter_context(nc.semaphore(name))

        ident = sb("ident", [P, P])
        ident_r = sb("ident_r", [P, P], F32R)
        x_raw = sb("x_raw", [P, TT, V])
        e_raw = sb("e_raw", [P, 2, KT * BN])
        w1_raw = sb("w1_raw", [P, 2, 2 * KT, P])
        w2_raw = sb("w2_raw", [P, 2, V])
        w1_hi, w1_lo = (sb(n, [P, 2, 2 * KT, P], F32R) for n in ("w1_hi", "w1_lo"))
        w2_hi, w2_lo = (sb(n, [P, 2, V], F32R) for n in ("w2_hi", "w2_lo"))
        aw_hi, aw_lo = (sb(n, [P, 2, KT * V], F32R) for n in ("aw_hi", "aw_lo"))
        x_hi, x_lo = (sb(n, [P, KT, TB], F32R) for n in ("x_hi", "x_lo"))
        ya_hi, ya_lo = (sb(n, [P, KT, TB], F32R) for n in ("ya_hi", "ya_lo"))
        vc_hi, vc_lo = (sb(n, [P, KT, TB], F32R) for n in ("vc_hi", "vc_lo"))
        xp_hi, xp_lo = (sb(n, [P, KT, TB], F32R) for n in ("xp_hi", "xp_lo"))
        resid = sb("resid", [P, KT, TB])
        probs = sb("probs", [P, TT, T])
        pT_hi, pT_lo = (sb(n, [P, SEQ, TS * T], F32R) for n in ("pT_hi", "pT_lo"))
        h3_hi, h3_lo = (sb(n, [P, MT, TB], F32R) for n in ("h3_hi", "h3_lo"))
        gel = sb("gel", [P, 2, TB])
        hid_hi, hid_lo = (sb(n, [P, 2, TB], F32R) for n in ("hid_hi", "hid_lo"))
        ln_p = sb("ln_p", [P, SEQ, 3, V])
        z01 = sb("z01", [P, 2, V])
        bias = sb("bias", [P, NROW])
        bd_all = sb("bd_all", [P, B * MT])
        bd_cur = sb("bd_cur", [P, SEQ * MT])
        codes_i = sb("codes_i", [P, B], I32)
        codes_f = sb("codes_f", [P, B])
        feat_i = sb("feat_i", [P, KT], I32)
        feat_f = sb("feat_f", [P, KT])
        cb_all = sb("cb_all", [P, NB, KT, SEQ])
        cb_cur = sb("cb_cur", [P, KT, SEQ])
        exp_i = sb("exp_i", [1, B], I32)
        exp_n = sb("exp_n", [1, B])
        exp_f = sb("exp_f", [1, B])
        exp_id = sb("exp_id", [1, B], I32)
        mx = sb("mx", [P, TT])
        nmx = sb("nmx", [P, TT])
        rsum = sb("rsum", [P, TT])
        rinv = sb("rinv", [P, TT])
        stat = sb("stat", [P, TT, 6])
        mv = sb("mv", [P, TT, 2])
        veps = sb("veps", [P, TT])
        rstd = sb("rstd", [P, TT])
        mhalf = sb("mhalf", [P, 1])

        z23 = probs[:, :, :].rearrange("p (z a) t -> p z (a t)", z=2)
        z = [z01[:, 0, :], z01[:, 1, :], z23[:, 0, :], z23[:, 1, :]]
        bias_rows = gel[0:NROW, 0, 0:P]
        bd_rows = z01[0:MT, :, :].rearrange("p a n -> p (a n)")
        wp_raw = w1_raw[:, :, :, :].rearrange("p a k n -> p (a k n)").rearrange("p (k n) -> p k n", k=KT)
        wk_raw = e_raw[:, :, :].rearrange("p a n -> p (a n)").rearrange("p (k n) -> p k n", k=KT)
        ps = [ctx.enter_context(nc.psum_tensor(f"bank{i}", [P, 512], F32)) for i in range(8)]

        fold_in = [sem(f"fold_in{i}") for i in range(4)]
        bias_in, codes_in, experts_in, bd_in = sem("bias_in"), sem("codes_in"), sem("experts_in"), sem("bd_in")
        x_in, e_in, proj_in, ln_in, proj_out = sem("x_in"), sem("e_in"), sem("proj_in"), sem("ln_in"), sem("proj_out")
        w1_in = [sem(f"w1_in{s}") for s in range(2)]
        w2_in = [sem(f"w2_in{s}") for s in range(2)]
        e1_in, z_free = sem("e1_in"), sem("z_free")
        stored = [sem(f"stored{t}") for t in range(TT)]
        bias_mm, tr_mm, fold_mm = sem("bias_mm"), sem("tr_mm"), sem("fold_mm")
        y_mm, v_mm, s_mm, down_mm, pT_mm, pv_mm, up_mm = (sem(n) for n in (
            "y_mm", "v_mm", "s_mm", "down_mm", "pT_mm", "pv_mm", "up_mm"))
        l1_mm, l2_mm = sem("l1_mm"), sem("l2_mm")
        tr_hi, fold_hi, y_hi, v_hi, pT_h, ao_hi, cms_hi, xp_h, e_hi, h3_h, w1_h, w2_h, gelu_done, exp_done, wp_h = (
            sem(n) for n in ("tr_hi", "fold_hi", "y_hi", "v_hi", "pT_h", "ao_hi", "cms_hi", "xp_h", "e_hi",
                             "h3_h", "w1_h", "w2_h", "gelu_done", "exp_done", "wp_h"))
        tr_lo, fold_lo, y_lo, v_lo, pT_l, ao_lo, cms_lo, xp_l, e_lo, h3_l, w1_l, w2_l, hid_l, wp_l = (
            sem(n) for n in ("tr_lo", "fold_lo", "y_lo", "v_lo", "pT_l", "ao_lo", "cms_lo", "xp_l", "e_lo",
                             "h3_l", "w1_l", "w2_l", "hid_l", "wp_l"))
        consts, iotas, bias_ready, ids_step, ids_ready, cb_step, cur_bias = (sem(n) for n in (
            "consts", "iotas", "bias_ready", "ids_step", "ids_ready", "cb_step", "cur_bias"))
        ident_ready, max_done, nmax_done, rinv_done, probs_done = (sem(n) for n in (
            "ident_ready", "max_done", "nmax_done", "rinv_done", "probs_done"))
        sum_done, clip_done, z_sum, ln_step, rstd_done, z_norm, z_scaled, resid_done = (sem(n) for n in (
            "sum_done", "clip_done", "z_sum", "ln_step", "rstd_done", "z_norm", "z_scaled", "resid_done"))
        L1_0, L2_0, HID_0, GELU_0, Z_0, Z_FREE_0 = 2, 2 * KT, 2, UNR, TT, 1

        def mm3(dst, w_hi, w_lo, a_hi, a_lo, start, stop, **kw):
            nc.tensor.matmul(dst, w_lo, a_hi, start=start, stop=False, **kw)
            nc.tensor.matmul(dst, w_hi, a_hi, start=False, stop=False, **kw)
            return nc.tensor.matmul(dst, w_hi, a_lo, start=False, stop=stop, **kw)

        def pe_transpose(src, bank0):
            for k in range(KT):
                for t in range(KT):
                    last = nc.tensor.transpose(ps[bank0 + k][:, t * P:(t + 1) * P],
                                               src[:, t, k * P:(k + 1) * P], ident[:, :])
                last.then_inc(tr_mm, 1)

        def pe_attention_1(pe, n, first):
            pe.wait_ge(x_in, 16 * (n + 1))
            if first:
                pe.wait_ge(fold_lo, KT)
            pe_transpose(x_raw, 4)
            if first:
                pe.wait_ge(fold_lo, 2 * KT)
            else:
                pe.wait_ge(sum_done, n * KT)
                pe.wait_ge(proj_in, n * 64)
            for k in range(KT):
                pe.wait_ge(tr_lo, 12 + n * KT + k + 1)
                for j in range(KT):
                    last = mm3(ps[j][:, :], aw_hi[:, 0, k * V + j * P:k * V + (j + 1) * P],
                               aw_lo[:, 0, k * V + j * P:k * V + (j + 1) * P],
                               x_hi[:, k, :], x_lo[:, k, :], k == 0, k == KT - 1)
                    if k == KT - 1:
                        last.then_inc(y_mm, 1)
            for t in range(TT):
                for k in range(KT):
                    last = mm3(ps[4 + t][:, :], x_hi[:, k, t * P:(t + 1) * P], x_lo[:, k, t * P:(t + 1) * P],
                               aw_hi[:, 1, k * V:(k + 1) * V], aw_lo[:, 1, k * V:(k + 1) * V],
                               k == 0, k == KT - 1)
                last.then_inc(v_mm, 1)
            pe.wait_ge(y_lo, n * KT + KT)
            for t in range(TT):
                seq = slice(t // TS * T, (t // TS + 1) * T)
                for k in range(KT):
                    last = mm3(ps[t][:, 0:T], ya_hi[:, k, t * P:(t + 1) * P], ya_lo[:, k, t * P:(t + 1) * P],
                               x_hi[:, k, seq], x_lo[:, k, seq], k == 0, k == KT - 1)
                last.then_inc(s_mm, 1)

        def pe_attention_2(pe, n):
            pe.wait_ge(v_lo, n * TT + TT)
            for b in range(SEQ):
                for s in range(TS):
                    pe.wait_ge(probs_done, n * TT + b * TS + s + 1)
                for u in range(TS):
                    for s in range(TS):
                        last = nc.tensor.transpose(ps[6 + b][:, u * T + s * P:u * T + (s + 1) * P],
                                                   probs[:, b * TS + s, u * P:(u + 1) * P], ident[:, :])
                last.then_inc(pT_mm, 1)
            pe.wait_ge(pT_l, n * SEQ + SEQ)
            for e in range(KT):
                for b in range(SEQ):
                    for u in range(TS):
                        w = b * TS + u
                        last = mm3(ps[e][:, b * T:(b + 1) * T], vc_hi[:, w, e * P:(e + 1) * P],
                                   vc_lo[:, w, e * P:(e + 1) * P], pT_hi[:, b, u * T:(u + 1) * T],
                                   pT_lo[:, b, u * T:(u + 1) * T], u == 0, u == TS - 1)
                last.then_inc(pv_mm, 1)

        def pe_down(pe, n, last):
            pe.wait_ge(xp_l, n + 1)
            pe.wait_ge(e_lo, n * SEQ + SEQ)
            if not last:
                pe.wait_ge(v_lo, n * TT + 2 * TT)
            for m in range(MT):
                for b in range(SEQ):
                    for k in range(KT):
                        w = slice(k * BN + m * P, k * BN + (m + 1) * P)
                        last = mm3(ps[4 + m][:, b * T:(b + 1) * T], aw_hi[:, b, w], aw_lo[:, b, w],
                                   xp_hi[:, k, b * T:(b + 1) * T], xp_lo[:, k, b * T:(b + 1) * T],
                                   k == 0, k == KT - 1)
                last.then_inc(down_mm, 1)

        def pe_up(pe, n):
            pe.wait_ge(h3_l, n * MT + MT)
            for t in range(TT):
                b, tok = t // TS, slice(t * P, (t + 1) * P)
                for m in range(MT):
                    w = slice(KT * BN + m * V, KT * BN + (m + 1) * V)
                    mm3(ps[4 + t][:, :], h3_hi[:, m, tok], h3_lo[:, m, tok], aw_hi[:, b, w], aw_lo[:, b, w],
                        m == 0, False)
                for k in range(KT):
                    dst = ps[4 + t][:, k * P:(k + 1) * P]
                    nc.tensor.matmul(dst, xp_hi[:, k, tok], ident_r[:, :], start=False, stop=False)
                    last = nc.tensor.matmul(dst, xp_lo[:, k, tok], ident_r[:, :], start=False, stop=k == KT - 1)
                last.then_inc(up_mm, 1)

        def pe_mlp(pe, n, phase):
            src = ((ya_hi, ya_lo, 0), (vc_hi, vc_lo, KT))

            def l1(q, g, part):
                a_hi, a_lo, k0 = src[part]
                for k in range(KT):
                    if part == 1:
                        pe.wait_ge(cms_lo, n * KT + k + 1)
                    last = mm3(ps[4 + q][:, :], w1_hi[:, q % 2, k0 + k, :], w1_lo[:, q % 2, k0 + k, :],
                               a_hi[:, k, :], a_lo[:, k, :], k0 + k == 0, part == phase and k == KT - 1)
                if part == phase:
                    last.then_inc(l1_mm, 1)

            def begin(q, g):
                pe.wait_ge(w1_l, g + 1)
                pe.wait_ge(gelu_done, g - UNR + 1 + GELU_0)
                if phase == 0:
                    pe.wait_ge(z_sum, n * TT + q % TT + 1)
                l1(q, g, 0)

            def l2(q, g, c):
                pe.wait_ge(w2_l, g + 1)
                pe.wait_ge(hid_l, g + 1 + HID_0)
                for j in range(KT):
                    w = slice(j * P, (j + 1) * P)
                    mm3(ps[j][:, :], w2_hi[:, q % 2, w], w2_lo[:, q % 2, w], hid_hi[:, q % 2, :],
                        hid_lo[:, q % 2, :], c, True, skip_group_check=True).then_inc(l2_mm, 1)

            def turn(g0, first):
                g = [g0 + q for q in range(UNR)]
                begin(0, g[0])
                begin(1, g[1])
                if phase:
                    l1(0, g[0], 1)
                    l1(1, g[1], 1)
                l2(0, g[0], first)
                for q in range(2, UNR):
                    begin(q, g[q])
                    if phase:
                        l1(q, g[q], 1)
                    l2(q - 1, g[q - 1], False)
                l2(UNR - 1, g[UNR - 1], False)

            base = n * CH + phase * NCH
            turn(base, True)
            with pe.Fori(1, ITS) as it:
                turn(base + it * UNR, False)

        def pe_program(pe):
            pe.sem_inc(l1_mm, L1_0)
            pe.sem_inc(l2_mm, L2_0)
            pe.wait_ge(ident_ready, 1)
            pe.wait_ge(fold_in[0], 16)
            pe_transpose(x_raw, 0)
            pe.wait_ge(bias_in, 16 * len(BIAS))
            nc.tensor.transpose(ps[7][:, 0:NROW], bias_rows[0:NROW, :], ident[0:NROW, 0:NROW])
            pe.wait_ge(bd_in, 16 * B)
            for b in range(B):
                last = nc.tensor.transpose(ps[7][:, 64 + MT * b:64 + MT * (b + 1)],
                                           bd_rows[0:MT, b * P:(b + 1) * P], ident[0:MT, 0:MT])
            last.then_inc(bias_mm, 1)
            pe.wait_ge(fold_in[1], 16)
            pe.wait_ge(bias_ready, 2)
            pe_transpose(wk_raw, 4)
            pe.wait_ge(fold_in[2], 16)
            pe.wait_ge(tr_lo, KT)
            pe_transpose(resid, 0)
            pe.wait_ge(tr_lo, 2 * KT)
            for m in range(KT):
                for k in range(KT):
                    last = mm3(ps[4 + m][:, :], ya_hi[:, k, m * P:(m + 1) * P], ya_lo[:, k, m * P:(m + 1) * P],
                               vc_hi[:, k, :], vc_lo[:, k, :], k == 0, k == KT - 1)
                last.then_inc(fold_mm, 1)
            pe.wait_ge(tr_lo, 3 * KT)
            pe.wait_ge(wp_l, 1)
            for m in range(KT):
                for k in range(KT):
                    last = mm3(ps[m][:, :], xp_hi[:, k, m * P:(m + 1) * P], xp_lo[:, k, m * P:(m + 1) * P],
                               x_hi[:, k, :], x_lo[:, k, :], k == 0, k == KT - 1)
                last.then_inc(fold_mm, 1)
            pe_attention_1(pe, 0, True)
            pe_attention_2(pe, 0)

            def mlps(n):
                pe.wait_ge(ao_lo, n * KT + KT)
                pe_mlp(pe, n, 0)
                pe_mlp(pe, n, 1)

            with pe.Fori(0, NB - 1) as n:
                mlps(n)
                pe_attention_1(pe, n + 1, False)
                pe_down(pe, n, False)
                pe_attention_2(pe, n + 1)
                pe_up(pe, n)
            mlps(NB - 1)
            pe_down(pe, NB - 1, True)
            pe_up(pe, NB - 1)

        def slot_views(phase, s):
            k = KIN[phase]
            return w1_hi[:, s, 0:k, :], w1_lo[:, s, 0:k, :], w1_raw[:, s, 0:k, :]

        def act_w1(act, phase, q, g, pair):
            act.wait_ge(w1_in[q % 2], 16 * pair + 16)
            act.wait_ge(l1_mm, g - 2 + 1 + L1_0)
            hi, _, raw = slot_views(phase, q % 2)
            nc.scalar.activation(hi, raw, ACT.Copy).then_inc(w1_h, 1)

        def act_w2(act, q, g, pair):
            act.wait_ge(w2_in[q % 2], 16 * pair + 16)
            act.wait_ge(l2_mm, (g - 2 + 1) * KT + L2_0)
            nc.scalar.activation(w2_hi[:, q % 2, :], w2_raw[:, q % 2, :], ACT.Copy).then_inc(w2_h, 1)

        def act_gelu(act, phase, q, g, col):
            act.wait_ge(l1_mm, g + 1 + L1_0)
            act.wait_ge(l2_mm, (g - 2 + 1) * KT + L2_0)
            act.wait_ge(hid_l, g - 2 + 1 + HID_0)
            b = bias[:, bass.ds(MLP_B[phase] + col, 1)] if not isinstance(col, int) else \
                bias[:, MLP_B[phase] + col:MLP_B[phase] + col + 1]
            nc.scalar.activation(hid_hi[:, q % 2, :], ps[4 + q][:, :], ACT.Gelu, bias=b)
            nc.scalar.activation(gel[:, q % 2, :], ps[4 + q][:, :], ACT.Gelu, bias=b).then_inc(gelu_done, 1)

        def chunk_steps(phase, n, it, last, w1, w2, gelu):
            q0 = phase * NCH
            g0 = n * CH + q0 + it * UNR
            h0 = n * NCH + (q0 + it * UNR) // 2 if isinstance(it, int) else n * NCH + q0 // 2 + it * (UNR // 2)
            nxt = 1 if last and phase == 0 else (0 if last else phase)
            w1n = lambda q: w1(nxt if q >= UNR else phase, q % UNR, g0 + q, h0 + q // 2)
            w2n = lambda q: w2(q % UNR, g0 + q, h0 + q // 2)
            more = not (last and phase == 1 and isinstance(n, int))
            col = it * UNR
            gelu(phase, 0, g0, col)
            w1n(2)
            gelu(phase, 1, g0 + 1, col + 1)
            w1n(3)
            w2n(2)
            gelu(phase, 2, g0 + 2, col + 2)
            w2n(3)
            if more:
                w1n(4)
            gelu(phase, 3, g0 + 3, col + 3)
            if more:
                w2n(4)
                w1n(5)
                if not last:
                    w2n(5)

        def act_tiles(act, mm, n0, banks, hi, sem_out, func=ACT.Copy, width=512, **kw):
            for k, bank in enumerate(banks):
                act.wait_ge(mm, n0 + k + 1)
                nc.scalar.activation(hi[:, k, :], ps[bank][:, :], func,
                                     **{a: f(k) for a, f in kw.items()}).then_inc(sem_out, 1)

        def act_attention_1(act, n, first):
            if not first:
                act.wait_ge(resid_done, n * 3)
            act_tiles(act, tr_mm, 12 + n * KT, range(4, 8), x_hi, tr_hi)
            act_tiles(act, y_mm, n * KT, range(4), ya_hi, y_hi)

        def act_softmax(act, n):
            act_tiles(act, v_mm, n * KT, range(4, 8), vc_hi, v_hi)

        def act_exps(act, n):
            act.wait_ge(nmax_done, n + 1)
            if not isinstance(n, int):
                act.wait_ge(z_free, n)
            for t in range(TT):
                nc.scalar.activation(probs[:, t, :], ps[t][:, 0:T], ACT.Exp, bias=nmx[:, t:t + 1], scale=SCALE,
                                     accum_out=rsum[:, t:t + 1]).then_inc(exp_done, 1)

        def act_attention_2(act, n):
            for b in range(SEQ):
                act.wait_ge(pT_mm, n * SEQ + b + 1)
                nc.scalar.activation(pT_hi[:, b, :], ps[6 + b][:, :], ACT.Copy).then_inc(pT_h, 1)
            act_tiles(act, pv_mm, n * KT, range(4), ya_hi, ao_hi, ACT.Identity,
                      bias=lambda k: bias[:, BP + k:BP + k + 1])

        def act_expert_weights(act, n, b):
            act.wait_ge((e_in, e1_in)[b], 32 * n + 32)
            nc.scalar.activation(aw_hi[:, b, :], e_raw[:, :, :].rearrange("p a n -> p (a n)"), ACT.Copy)\
                .then_inc(e_hi, 1)

        def act_down(act, n):
            for m in range(MT):
                act.wait_ge(down_mm, n * MT + m + 1)
                for b in range(SEQ):
                    col, cols = bd_cur[:, b * MT + m:b * MT + m + 1], slice(b * T, (b + 1) * T)
                    nc.scalar.activation(h3_hi[:, m, cols], ps[4 + m][:, cols], ACT.Gelu, bias=col)
                    last = nc.scalar.activation(gel[:, m, cols], ps[4 + m][:, cols], ACT.Gelu, bias=col)
                last.then_inc(h3_h, 1)

        def act_xp(act, n):
            act.wait_ge(clip_done, n + 1)
            nc.scalar.activation(xp_hi[:, :, :], resid[:, :, :], ACT.Copy).then_inc(xp_h, 1)

        def act_program(act):
            act.sem_inc(gelu_done, GELU_0)
            at = 0
            for (src, n), off in zip(BIAS, offs):
                act.dma_start(bias_rows[off:off + n // P, :], src.rearrange("(r p) -> r p", p=P)).then_inc(bias_in, 16)
            act_tiles(act, tr_mm, 0, range(4), ya_hi, tr_hi)
            act_tiles(act, tr_mm, KT, range(4, 8), vc_hi, tr_hi)
            act_tiles(act, tr_mm, 2 * KT, range(4), xp_hi, tr_hi)
            act.wait_ge(fold_in[3], 16)
            nc.scalar.activation(x_hi[:, :, :], wp_raw, ACT.Copy).then_inc(wp_h, 1)
            for slot, banks in ((0, range(4, 8)), (1, range(4))):
                for m, bank in enumerate(banks):
                    act.wait_ge(fold_mm, slot * KT + m + 1)
                    nc.scalar.activation(aw_hi[:, slot, m * V:(m + 1) * V], ps[bank][:, :], ACT.Copy)\
                        .then_inc(fold_hi, 1)
            act_attention_1(act, 0, True)
            act_w1(act, 0, 0, 0, 0)
            act_w2(act, 0, 0, 0)
            act_softmax(act, 0)
            act_w1(act, 0, 1, 1, 0)
            act_w2(act, 1, 1, 0)
            act_exps(act, 0)
            act_attention_2(act, 0)

            def mlps(n):
                for phase in range(2):
                    steps = lambda it, last: chunk_steps(
                        phase, n, it, last, lambda ph, q, g, h: act_w1(act, ph, q, g, h),
                        lambda q, g, h: act_w2(act, q, g, h), lambda ph, q, g, c: act_gelu(act, ph, q, g, c))
                    with act.Fori(0, ITS - 1) as it:
                        steps(it, False)
                    steps(ITS - 1, True)
                    if phase == 0:
                        act.wait_ge(cur_bias, n * 2 + 2)
                        for j in range(KT):
                            act.wait_ge(l2_mm, (n * CH + NCH - 1) * KT + j + 1 + L2_0)
                            for b in range(SEQ):
                                cols = slice(b * T, (b + 1) * T)
                                last = nc.scalar.activation(vc_hi[:, j, cols], ps[j][:, cols], ACT.Identity,
                                                            bias=cb_cur[:, j, b:b + 1])
                            last.then_inc(cms_hi, 1)
                        act_w2(act, 1, n * CH + NCH + 1, n * NCH + NCH // 2)

            with act.Fori(0, NB - 1) as n:
                mlps(n)
                act_attention_1(act, n + 1, False)
                act_w2(act, 1, n * CH + CH + 1, n * NCH + NCH)
                act_expert_weights(act, n, 0)
                act_xp(act, n)
                act_softmax(act, n + 1)
                act_expert_weights(act, n, 1)
                act_exps(act, n + 1)
                act_down(act, n)
                act_attention_2(act, n + 1)
            mlps(NB - 1)
            act_expert_weights(act, NB - 1, 0)
            act_expert_weights(act, NB - 1, 1)
            act_xp(act, NB - 1)
            act_down(act, NB - 1)

        sub = lambda dst, a, hi: nc.vector.tensor_tensor(dst, a, hi.bitcast(F32), ALU.subtract)

        def dve_w1(dve, phase, q, g, pair):
            dve.wait_ge(w1_h, g + 1)
            hi, lo, raw = slot_views(phase, q % 2)
            sub(lo, raw, hi).then_inc(w1_l, 1)

        def dve_w2(dve, q, g, pair):
            dve.wait_ge(w2_h, g + 1)
            sub(w2_lo[:, q % 2, :], w2_raw[:, q % 2, :], w2_hi[:, q % 2, :]).then_inc(w2_l, 1)

        def dve_gelu(dve, phase, q, g, col):
            dve.wait_ge(gelu_done, g + 1 + GELU_0)
            sub(hid_lo[:, q % 2, :], gel[:, q % 2, :], hid_hi[:, q % 2, :]).then_inc(hid_l, 1)

        def dve_tiles(dve, hi_sem, n0, banks, hi, lo, lo_sem):
            for k, bank in enumerate(banks):
                dve.wait_ge(hi_sem, n0 + k + 1)
                sub(lo[:, k, :], ps[bank][:, :], hi[:, k, :]).then_inc(lo_sem, 1)

        def dve_attention_1(dve, n):
            dve_tiles(dve, tr_hi, 12 + n * KT, range(4, 8), x_hi, x_lo, tr_lo)

        def dve_y(dve, n):
            dve_tiles(dve, y_hi, n * KT, range(4), ya_hi, ya_lo, y_lo)

        def dve_v(dve, n):
            dve_tiles(dve, v_hi, n * KT, range(4, 8), vc_hi, vc_lo, v_lo)

        def dve_softmax(dve, n):
            for t in range(TT):
                dve.wait_ge(s_mm, n * TT + t + 1)
                nc.vector.reduce_max(mx[:, t:t + 1], ps[t][:, 0:T], AX_X).then_inc(max_done, 1)
            dve.wait_ge(max_done, n * TT + TT)
            nc.vector.tensor_scalar_mul(nmx[:, :], mx[:, :], -SCALE).then_inc(nmax_done, 1)

        def dve_probs(dve, n):
            dve.wait_ge(exp_done, n * TT + TT)
            nc.vector.reciprocal(rinv[:, :], rsum[:, :]).then_inc(rinv_done, 1)
            dve.wait_ge(rinv_done, n + 1)
            for t in range(TT):
                nc.vector.tensor_scalar_mul(probs[:, t, :], probs[:, t, :], rinv[:, t:t + 1])\
                    .then_inc(probs_done, 1)

        def dve_attention_2(dve, n):
            for b in range(SEQ):
                dve.wait_ge(pT_h, n * SEQ + b + 1)
                sub(pT_lo[:, b, :], ps[6 + b][:, :], pT_hi[:, b, :]).then_inc(pT_l, 1)
            for e in range(KT):
                dve.wait_ge(ao_hi, n * KT + e + 1)
                nc.vector.scalar_tensor_tensor(out=ya_lo[:, e, :], in0=ps[e][:, :], scalar=bias[:, BP + e:BP + e + 1],
                                               in1=ya_hi[:, e, :].bitcast(F32), op0=ALU.add, op1=ALU.subtract)\
                    .then_inc(ao_lo, 1)

        def dve_expert_weights(dve, n, b):
            dve.wait_ge(e_hi, n * SEQ + b + 1)
            sub(aw_lo[:, b, :], e_raw[:, :, :].rearrange("p a n -> p (a n)"), aw_hi[:, b, :]).then_inc(e_lo, 1)

        def dve_sum(dve, n):
            dve.wait_ge(resid_done, n * 3 + 3)
            for j in range(KT):
                dve.wait_ge(l2_mm, (n * CH + CH - 1) * KT + j + 1 + L2_0)
                nc.vector.scalar_tensor_tensor(out=resid[:, j, :], in0=ps[j][:, :], scalar=bias[:, MB2 + j:MB2 + j + 1],
                                               in1=resid[:, j, :], op0=ALU.add, op1=ALU.add).then_inc(sum_done, 1)

        def dve_clip(dve, n):
            dve.wait_ge(sum_done, n * KT + KT)
            nc.vector.tensor_scalar(resid[:, :, :], resid[:, :, :], 0.0, 1.0, ALU.max, ALU.min).then_inc(clip_done, 1)

        def dve_xp(dve, n):
            dve.wait_ge(xp_h, n + 1)
            sub(xp_lo[:, :, :], resid[:, :, :], xp_hi[:, :, :]).then_inc(xp_l, 1)

        def dve_h3(dve, n):
            for m in range(MT):
                dve.wait_ge(h3_h, n * MT + m + 1)
                sub(h3_lo[:, m, :], gel[:, m, :], h3_hi[:, m, :]).then_inc(h3_l, 1)

        def dve_layer_norm(dve, n):
            def stats(t):
                dve.wait_ge(up_mm, n * TT + t + 1)
                if t == 0:
                    dve.wait_ge(ln_in, 16 * 3 * SEQ * (n + 1))
                dve.wait_ge(z_free, n + Z_FREE_0)
                nc.vector.tensor_tensor(z[t], ps[4 + t][:, :], ln_p[:, t // TS, 0, :], ALU.add).then_inc(z_sum, 1)
                s = n * 3 * TT + 3 * t
                dve.wait_ge(z_sum, n * TT + t + 1 + Z_0)
                nc.vector.bn_stats(stat[:, t, :], z[t]).then_inc(ln_step, 1)
                dve.drain()
                nc.vector.bn_aggr(mv[:, t, :], stat[:, t, :]).then_inc(ln_step, 1)
                dve.wait_ge(ln_step, s + 2)
                nc.vector.tensor_scalar_add(veps[:, t:t + 1], mv[:, t, 1:2], LN_EPS).then_inc(ln_step, 1)

            def norm(t):
                dve.wait_ge(rstd_done, n * TT + t + 1)
                nc.vector.tensor_scalar(z[t], z[t], mv[:, t, 0:1], rstd[:, t:t + 1], ALU.subtract, ALU.mult)\
                    .then_inc(z_norm, 1)

            stats(0)
            for t in range(1, TT):
                stats(t)
                norm(t - 1)
            norm(TT - 1)

        def dve_columns(n):
            nc.vector.tensor_copy(bd_cur[:, :], bd_all[:, bass.ds(n * (SEQ * MT), SEQ * MT)]).then_inc(cur_bias, 1)
            flat = cb_all[:, :, :, :].rearrange("p n k s -> p (n k s)")
            nc.vector.tensor_copy(cb_cur[:, :, :].rearrange("p k s -> p (k s)"),
                                  flat[:, bass.ds(n * (KT * SEQ), KT * SEQ)]).then_inc(cur_bias, 1)

        def dve_program(dve):
            dve.sem_inc(hid_l, HID_0)
            dve.sem_inc(z_sum, Z_0)
            nc.vector.memset(mhalf[:, :], -0.5).then_inc(consts, 1)
            dve.wait_ge(experts_in, 16)
            nc.vector.tensor_scalar(exp_n[:, :], exp_i[:, :], 0.0, float(E), ALU.is_lt, ALU.mult).then_inc(ids_step, 1)
            dve.wait_ge(ids_step, 1)
            nc.vector.tensor_tensor(exp_f[:, :], exp_n[:, :], exp_i[:, :], ALU.add).then_inc(ids_step, 1)
            dve.wait_ge(ids_step, 2)
            nc.vector.tensor_scalar(exp_id[:, :], exp_f[:, :], 0.0, float(E - 1), ALU.max, ALU.min)\
                .then_inc(ids_ready, 1)
            dve.wait_ge(ident_ready, 1)
            nc.vector.tensor_copy(ident_r[:, :], ident[:, :]).then_inc(consts, 1)
            dve_tiles(dve, tr_hi, 0, range(4), ya_hi, ya_lo, tr_lo)
            dve.wait_ge(bias_mm, 1)
            nc.vector.tensor_copy(bias[:, :], ps[7][:, 0:NROW]).then_inc(bias_ready, 1)
            nc.vector.tensor_copy(bd_all[:, :], ps[7][:, 64:64 + B * MT]).then_inc(bias_ready, 1)
            dve.wait_ge(codes_in, 16)
            dve.wait_ge(iotas, 1)
            nc.vector.tensor_copy(codes_f[:, :], codes_i[:, :]).then_inc(cb_step, 1)
            nc.vector.tensor_copy(feat_f[:, :], feat_i[:, :]).then_inc(cb_step, 1)
            dve.wait_ge(cb_step, 2)
            dve.wait_ge(bias_ready, 2)
            for k in range(KT):
                nc.vector.tensor_scalar(cb_all[:, :, k, :], codes_f[:, :].rearrange("p (n s) -> p n s", s=SEQ),
                                        feat_f[:, k:k + 1], bias[:, CB2 + k:CB2 + k + 1], ALU.is_equal, ALU.add)\
                    .then_inc(cb_step, 1)
            dve.wait_ge(cb_step, 2 + KT)
            dve_tiles(dve, tr_hi, KT, range(4, 8), vc_hi, vc_lo, tr_lo)
            dve_tiles(dve, tr_hi, 2 * KT, range(4), xp_hi, xp_lo, tr_lo)
            dve.wait_ge(wp_h, 1)
            sub(x_lo[:, :, :], wp_raw, x_hi[:, :, :]).then_inc(wp_l, 1)
            for slot, banks in ((0, range(4, 8)), (1, range(4))):
                for m, bank in enumerate(banks):
                    dve.wait_ge(fold_hi, slot * KT + m + 1)
                    cols = slice(m * V, (m + 1) * V)
                    sub(aw_lo[:, slot, cols], ps[bank][:, :], aw_hi[:, slot, cols]).then_inc(fold_lo, 1)
            dve_attention_1(dve, 0)
            dve_y(dve, 0)
            dve_w1(dve, 0, 0, 0, 0)
            dve_w2(dve, 0, 0, 0)
            dve_v(dve, 0)
            dve_w1(dve, 0, 1, 1, 0)
            dve_w2(dve, 1, 1, 0)
            dve_softmax(dve, 0)
            dve_probs(dve, 0)
            dve_attention_2(dve, 0)

            def mlps(n):
                dve_columns(n)
                for phase in range(2):
                    steps = lambda it, last: chunk_steps(
                        phase, n, it, last, lambda ph, q, g, h: dve_w1(dve, ph, q, g, h),
                        lambda q, g, h: dve_w2(dve, q, g, h), lambda ph, q, g, c: dve_gelu(dve, ph, q, g, c))
                    with dve.Fori(0, ITS - 1) as it:
                        steps(it, False)
                    steps(ITS - 1, True)
                    if phase == 0:
                        dve.wait_ge(cur_bias, n * 2 + 2)
                        for j in range(KT):
                            dve.wait_ge(cms_hi, n * KT + j + 1)
                            for b in range(SEQ):
                                cols = slice(b * T, (b + 1) * T)
                                last = nc.vector.scalar_tensor_tensor(
                                    out=vc_lo[:, j, cols], in0=ps[j][:, cols], scalar=cb_cur[:, j, b:b + 1],
                                    in1=vc_hi[:, j, cols].bitcast(F32), op0=ALU.add, op1=ALU.subtract)
                            last.then_inc(cms_lo, 1)
                        dve_w2(dve, 1, n * CH + NCH + 1, 0)

            with dve.Fori(0, NB - 1) as n:
                mlps(n)
                dve_sum(dve, n)
                dve_attention_1(dve, n + 1)
                dve_clip(dve, n)
                dve_y(dve, n + 1)
                dve_w2(dve, 1, n * CH + CH + 1, 0)
                dve_expert_weights(dve, n, 0)
                dve_xp(dve, n)
                dve_v(dve, n + 1)
                dve_expert_weights(dve, n, 1)
                dve_softmax(dve, n + 1)
                dve_probs(dve, n + 1)
                dve_h3(dve, n)
                dve_attention_2(dve, n + 1)
                dve_layer_norm(dve, n)
            mlps(NB - 1)
            dve_expert_weights(dve, NB - 1, 0)
            dve_expert_weights(dve, NB - 1, 1)
            dve_sum(dve, NB - 1)
            dve_clip(dve, NB - 1)
            dve_xp(dve, NB - 1)
            dve_h3(dve, NB - 1)
            dve_layer_norm(dve, NB - 1)

        def pool_residual(pool, n):
            pool.wait_ge(cms_lo, n * KT + KT)
            nc.gpsimd.tensor_tensor(resid[:, :, :], vc_hi[:, :, :].bitcast(F32), vc_lo[:, :, :].bitcast(F32),
                                    ALU.add).then_inc(resid_done, 1)
            pool.wait_ge(resid_done, n * 3 + 1)
            nc.gpsimd.tensor_tensor(resid[:, :, :], resid[:, :, :], x_hi[:, :, :].bitcast(F32), ALU.add)\
                .then_inc(resid_done, 1)
            pool.wait_ge(resid_done, n * 3 + 2)
            nc.gpsimd.tensor_tensor(resid[:, :, :], resid[:, :, :], x_lo[:, :, :].bitcast(F32), ALU.add)\
                .then_inc(resid_done, 1)

        def load_expert(eng, n, b, landed):
            e = eng.value_load(exp_id[0:1, bass.ds(n * SEQ + b, 1)], min_val=0, max_val=E - 1)
            eng.dma_start(e_raw[:, 0, :].rearrange("p (k n) -> p k n", k=KT),
                          down_v[:, bass.ds(e * KT, KT), :]).then_inc(landed, 16)
            eng.dma_start(e_raw[:, 1, :].rearrange("p (k n) -> p k n", k=MT),
                          up_v[:, bass.ds(e * MT, MT), :]).then_inc(landed, 16)

        def pool_expert(pool, n):
            pool.wait_ge(e_lo, n * SEQ + 1)
            load_expert(pool, n, 1, e1_in)

            def power(t):
                pool.wait_ge(ln_step, n * 3 * TT + 3 * t + 3)
                nc.gpsimd.tensor_tensor(rstd[:, t:t + 1], veps[:, t:t + 1], mhalf[:, :], ALU.pow)\
                    .then_inc(rstd_done, 1)

            def scale_and_store(t):
                s = n * 2 * TT + 2 * t
                pool.wait_ge(z_norm, n * TT + t + 1)
                nc.gpsimd.tensor_tensor(z[t], z[t], ln_p[:, t // TS, 1, :], ALU.mult).then_inc(z_scaled, 1)
                pool.wait_ge(z_scaled, s + 1)
                nc.gpsimd.tensor_tensor(z[t], z[t], ln_p[:, t // TS, 2, :], ALU.add).then_inc(z_scaled, 1)
                pool.wait_ge(z_scaled, s + 2)
                pool.dma_start(out_rows[bass.ds(n * TB + t * P, P), :], z[t]).then_inc(stored[t], 16)

            power(0)
            for t in range(1, TT):
                power(t)
                scale_and_store(t - 1)
            scale_and_store(TT - 1)
            for t in range(TT):
                pool.wait_ge(stored[t], 16 * n + 16)
            pool.sem_inc(z_free, 1)

        def pool_program(pool):
            pool.sem_inc(z_free, Z_FREE_0)
            nc.gpsimd.memset(ident[:, :], 0.0).then_inc(iotas, 1)
            nc.gpsimd.iota(feat_i[:, :], pattern=[[P, KT]], base=0, channel_multiplier=1).then_inc(iotas, 1)
            pool.wait_ge(iotas, 2)
            nc.gpsimd.affine_select(out=ident[:, :], in_=ident[:, :], compare_op=ALU.not_equal, fill=1.0, base=0,
                                    pattern=[[-1, P]], channel_multiplier=1).then_inc(ident_ready, 1)
            pool.wait_ge(ids_ready, 1)
            with pool.Fori(0, B) as b:
                e = pool.value_load(exp_id[0:1, bass.ds(b, 1)], min_val=0, max_val=E - 1)
                pool.dma_start(bd_rows[:, bass.ds(b * P, P)], bdown_v[bass.ds(e * MT, MT), :]).then_inc(bd_in, 16)
            pool.wait_ge(consts, 1)
            with pool.Fori(0, NB) as n:
                pool_residual(pool, n)
                pool_expert(pool, n)
            for s in stored:
                pool.wait_ge(s, 16 * NB)

        def load_chunk(sp, phase, s, g, c):
            k = KIN[phase]
            sp.dma_start(w1_raw[:, s, 0:k, :], mlp_w1[phase][:, :, bass.ds(c, P)]).then_inc(w1_in[s], 16)
            sp.dma_start(w2_raw[:, s, :], mlp_w2[phase][bass.ds(c, P), :]).then_inc(w2_in[s], 16)

        def load_aux(sp, n, more):
            sp.wait_ge(z_free, n + Z_FREE_0)
            if more:
                sp.wait_ge(tr_mm, 12 + n * KT + KT)
                sp.dma_start(x_raw[:, :, :], x_rows[bass.ds((n + 1) * TB, TB), :]
                             .rearrange("(t p) v -> p t v", p=P)).then_inc(x_in, 16)
                sp.wait_ge(v_mm, n * TT + TT)
                for slot in range(2):
                    sp.dma_start(aw_hi[:, slot, :].bitcast(F32), proj_hi[:, slot, :]).then_inc(proj_in, 16)
                    sp.dma_start(aw_lo[:, slot, :].bitcast(F32), proj_lo[:, slot, :]).then_inc(proj_in, 16)
            load_expert(sp, n, 0, e_in)
            for b in range(SEQ):
                e = sp.value_load(exp_id[0:1, bass.ds(n * SEQ + b, 1)], min_val=0, max_val=E - 1)
                for i, src in enumerate(ln_v):
                    sp.dma_start(ln_p[:, b, i, :], src[bass.ds(e, 1), :].to_broadcast([P, V])).then_inc(ln_in, 16)

        def sync_program(sp):
            sp.dma_start(exp_i[:, :], row_of(experts)).then_inc(experts_in, 16)
            sp.dma_start(x_raw[:, :, :], square[0]).then_inc(fold_in[0], 16)
            sp.dma_start(wk_raw, square[1]).then_inc(fold_in[1], 16)
            sp.dma_start(codes_i[:, :], row_of(codes).to_broadcast([P, B])).then_inc(codes_in, 16)
            sp.dma_start(resid[:, :, :], square[2]).then_inc(fold_in[2], 16)
            sp.dma_start(wp_raw, square[3]).then_inc(fold_in[3], 16)
            sp.wait_ge(tr_mm, KT)
            sp.dma_start(x_raw[:, :, :], x_rows[0:TB, :].rearrange("(t p) v -> p t v", p=P)).then_inc(x_in, 16)
            sp.wait_ge(wp_l, 1)
            load_chunk(sp, 0, 0, 0, 0)
            load_chunk(sp, 0, 1, 1, P)
            sp.wait_ge(fold_lo, 2 * KT)
            for slot in range(2):
                sp.dma_start(proj_hi[:, slot, :], aw_hi[:, slot, :].bitcast(F32)).then_inc(proj_out, 16)
                sp.dma_start(proj_lo[:, slot, :], aw_lo[:, slot, :].bitcast(F32)).then_inc(proj_out, 16)
            sp.wait_ge(ids_ready, 1)
            sp.wait_ge(proj_out, 64)

            def chunk_pair(phase, g, c):
                for s in range(2):
                    sp.wait_ge(w1_l, g + s - 1)
                    sp.wait_ge(w2_l, g + s - 1)
                    load_chunk(sp, phase, s, g + s, c + s * P)

            def mlps(n, more):
                with sp.Fori(1, NCH // 2) as j:
                    chunk_pair(0, n * CH + j * 2, j * (2 * P))
                load_aux(sp, n, more)
                with sp.Fori(0, NCH // 2) as j:
                    chunk_pair(1, n * CH + NCH + j * 2, j * (2 * P))
                if more:
                    chunk_pair(0, n * CH + CH, 0)

            with sp.Fori(0, NB - 1) as n:
                mlps(n, True)
            mlps(NB - 1, False)

        block = ctx.enter_context(nc.Block())

        @block.sync
        def _(sp):
            sync_program(sp)

        @block.gpsimd
        def _(pool):
            pool_program(pool)

        @block.scalar
        def _(act):
            act_program(act)

        @block.vector
        def _(dve):
            dve_program(dve)

        @block.tensor
        def _(pe):
            pe_program(pe)


_INS = ['x', 'itok_B_17_1546', 'itok_B_1_2', 'L0_cond_Wq', 'L0_cond_Wk', 'L0_cond_Wv', 'L0_cond_Wp', 'L0_cond_bp',
        'L0_cond_cW1', 'L0_cond_cb1', 'L0_cond_cW2', 'L0_cond_cb2', 'L0_cond_mW1', 'L0_cond_mb1', 'L0_cond_mW2',
        'L0_cond_mb2', 'L1_cond_W_down', 'L1_cond_b_down', 'L1_cond_W_up', 'L1_cond_b_up', 'L1_cond_ln_w',
        'L1_cond_ln_b']


def kernel(**inputs):
    import numpy as np
    import concourse.bacc as bacc
    from concourse.bass_utils import run_bass_kernel_spmd as run

    nc = bacc.Bacc("TRN2", target_bir_lowering=False, num_devices=1)
    arrays, args = {}, []
    for name in _INS:
        a = np.ascontiguousarray(inputs[name])
        arrays[f"in_{name}"] = a
        args.append(nc.dram_tensor(f"in_{name}", a.shape, mybir.dt.from_np(a.dtype), kind="ExternalInput").ap())
    shape = inputs['x'].shape
    args.append(nc.dram_tensor("out_0", shape, F32, kind="ExternalOutput").ap())
    build(nc, *args)
    r = run(nc, [arrays], core_ids=[0])
    return r.results[0]["out_0"]
```

```python
from contextlib import ExitStack

import concourse.bass as bass
from concourse import mybir

F32 = mybir.dt.float32
F32R = mybir.dt.float32r
I32 = mybir.dt.int32
ACT = mybir.ActivationFunctionType
ALU = mybir.AluOpType
AX_X = mybir.AxisListType.X

P = 128
LN_EPS = 1e-5


def build(nc, x, codes, experts, Wq, Wk, Wv, Wp, bp, cW1, cb1, cW2, cb2, mW1, mb1, mW2, mb2,
          W_down, b_down, W_up, b_up, ln_w, ln_b, out):
    B, T, V = x.shape
    H = cW1.shape[1]
    E, _, BN = W_down.shape
    SEQ = 2
    TB = SEQ * T
    NB = B // SEQ
    KT = V // P
    TT = TB // P
    TS = T // P
    MT = BN // P
    NCH = H // P
    CH = 2 * NCH
    UNR = 4
    ITS = NCH // UNR
    SCALE = float(V) ** -0.5
    KIN = (KT, 2 * KT)

    x_rows = x.rearrange("b t v -> (b t) v")
    out_rows = out.rearrange("b t v -> (b t) v")
    mlp_w1 = (cW1.rearrange("(k p) n -> p k n", p=P), mW1.rearrange("(k p) n -> p k n", p=P))
    mlp_w2 = (cW2, mW2)
    square = [w.rearrange("(k p) n -> p k n", p=P) for w in (Wq, Wk, Wv, Wp)]
    down_v = W_down.rearrange("e (k p) n -> p (e k) n", p=P)
    up_v = W_up.rearrange("e (k p) n -> p (e k) n", p=P)
    bdown_v = b_down.rearrange("e (m p) -> (e m) p", p=P)
    row_of = lambda a: a.rearrange("(o b) -> o b", o=1)
    ln_v = (b_up, ln_w, ln_b)
    proj_hi = nc.dram_tensor("proj_hi", (P, 2, KT * V), F32, kind="Internal").ap()
    proj_lo = nc.dram_tensor("proj_lo", (P, 2, KT * V), F32, kind="Internal").ap()

    BIAS = ((bp, V), (cb1, H), (cb2, V), (mb1, H), (mb2, V))
    at, offs = 0, []
    for _, n in BIAS:
        offs.append(at)
        at += n // P
    NROW = at
    BP, CB1, CB2, MB1, MB2 = offs
    MLP_B = (CB1, MB1)

    with ExitStack() as ctx:
        sb = lambda name, shape, dt=F32: ctx.enter_context(nc.sbuf_tensor(name, shape, dt))
        sem = lambda name: ctx.enter_context(nc.semaphore(name))

        ident = sb("ident", [P, P])
        ident_r = sb("ident_r", [P, P], F32R)
        x_raw = sb("x_raw", [P, TT, V])
        e_raw = sb("e_raw", [P, 2, KT * BN])
        w1_raw = sb("w1_raw", [P, 2, 2 * KT, P])
        w2_raw = sb("w2_raw", [P, 2, V])
        w1_hi, w1_lo = (sb(n, [P, 2, 2 * KT, P], F32R) for n in ("w1_hi", "w1_lo"))
        w2_hi, w2_lo = (sb(n, [P, 2, V], F32R) for n in ("w2_hi", "w2_lo"))
        aw_hi, aw_lo = (sb(n, [P, 2, KT * V], F32R) for n in ("aw_hi", "aw_lo"))
        x_hi, x_lo = (sb(n, [P, KT, TB], F32R) for n in ("x_hi", "x_lo"))
        ya_hi, ya_lo = (sb(n, [P, KT, TB], F32R) for n in ("ya_hi", "ya_lo"))
        vc_hi, vc_lo = (sb(n, [P, KT, TB], F32R) for n in ("vc_hi", "vc_lo"))
        xp_hi, xp_lo = (sb(n, [P, KT, TB], F32R) for n in ("xp_hi", "xp_lo"))
        resid = sb("resid", [P, KT, TB])
        probs = sb("probs", [P, TT, T])
        pT_hi, pT_lo = (sb(n, [P, SEQ, TS * T], F32R) for n in ("pT_hi", "pT_lo"))
        h3_hi, h3_lo = (sb(n, [P, MT, TB], F32R) for n in ("h3_hi", "h3_lo"))
        gel = sb("gel", [P, 2, TB])
        hid_hi, hid_lo = (sb(n, [P, 2, TB], F32R) for n in ("hid_hi", "hid_lo"))
        ln_p = sb("ln_p", [P, SEQ, 3, V])
        z01 = sb("z01", [P, 2, V])
        bias = sb("bias", [P, NROW])
        bd_all = sb("bd_all", [P, B * MT])
        bd_cur = sb("bd_cur", [P, SEQ * MT])
        codes_i = sb("codes_i", [P, B], I32)
        codes_f = sb("codes_f", [P, B])
        feat_i = sb("feat_i", [P, KT], I32)
        feat_f = sb("feat_f", [P, KT])
        cb_all = sb("cb_all", [P, NB, KT, SEQ])
        cb_cur = sb("cb_cur", [P, KT, SEQ])
        exp_i = sb("exp_i", [1, B], I32)
        exp_n = sb("exp_n", [1, B])
        exp_f = sb("exp_f", [1, B])
        exp_id = sb("exp_id", [1, B], I32)
        mx = sb("mx", [P, TT])
        nmx = sb("nmx", [P, TT])
        rsum = sb("rsum", [P, TT])
        rinv = sb("rinv", [P, TT])
        stat = sb("stat", [P, TT, 6])
        mv = sb("mv", [P, TT, 2])
        veps = sb("veps", [P, TT])
        rstd = sb("rstd", [P, TT])
        mhalf = sb("mhalf", [P, 1])
        warm = sb("warm", [P, 1])

        z23 = probs[:, :, :].rearrange("p (z a) t -> p z (a t)", z=2)
        z = [z01[:, 0, :], z01[:, 1, :], z23[:, 0, :], z23[:, 1, :]]
        bias_rows = gel[0:NROW, 0, 0:P]
        bd_rows = z01[0:MT, :, :].rearrange("p a n -> p (a n)")
        wp_raw = w1_raw[:, :, :, :].rearrange("p a k n -> p (a k n)").rearrange("p (k n) -> p k n", k=KT)
        wk_raw = e_raw[:, :, :].rearrange("p a n -> p (a n)").rearrange("p (k n) -> p k n", k=KT)
        ps = [ctx.enter_context(nc.psum_tensor(f"bank{i}", [P, 512], F32)) for i in range(8)]

        fold_in = [sem(f"fold_in{i}") for i in range(4)]
        bias_in, codes_in, experts_in, bd_in = sem("bias_in"), sem("codes_in"), sem("experts_in"), sem("bd_in")
        x_in, e_in, proj_in, ln_in, proj_out = sem("x_in"), sem("e_in"), sem("proj_in"), sem("ln_in"), sem("proj_out")
        w1_in = [sem(f"w1_in{s}") for s in range(2)]
        w2_in = [sem(f"w2_in{s}") for s in range(2)]
        z_last, last_step, stored_last = sem("z_last"), sem("last_step"), sem("stored_last")
        fold_q = [sem(f"fold_q{t}") for t in range(KT)]
        e1_in, z_free = sem("e1_in"), sem("z_free")
        stored = [sem(f"stored{t}") for t in range(TT)]
        bias_mm, tr_mm, fold_mm = sem("bias_mm"), sem("tr_mm"), sem("fold_mm")
        y_mm, v_mm, s_mm, down_mm, pT_mm, pv_mm, up_mm = (sem(n) for n in (
            "y_mm", "v_mm", "s_mm", "down_mm", "pT_mm", "pv_mm", "up_mm"))
        l1_mm, l2_mm = sem("l1_mm"), sem("l2_mm")
        tr_hi, fold_hi, y_hi, v_hi, pT_h, ao_hi, cms_hi, xp_h, e_hi, h3_h, w1_h, w2_h, gelu_done, exp_done, wp_h = (
            sem(n) for n in ("tr_hi", "fold_hi", "y_hi", "v_hi", "pT_h", "ao_hi", "cms_hi", "xp_h", "e_hi",
                             "h3_h", "w1_h", "w2_h", "gelu_done", "exp_done", "wp_h"))
        tr_lo, fold_lo, y_lo, v_lo, pT_l, ao_lo, cms_lo, xp_l, e_lo, h3_l, w1_l, w2_l, hid_l, wp_l = (
            sem(n) for n in ("tr_lo", "fold_lo", "y_lo", "v_lo", "pT_l", "ao_lo", "cms_lo", "xp_l", "e_lo",
                             "h3_l", "w1_l", "w2_l", "hid_l", "wp_l"))
        consts, iotas, bias_ready, ids_step, ids_ready, cb_step, cur_bias = (sem(n) for n in (
            "consts", "iotas", "bias_ready", "ids_step", "ids_ready", "cb_step", "cur_bias"))
        ident_ready, max_done, nmax_done, rinv_done, probs_done = (sem(n) for n in (
            "ident_ready", "max_done", "nmax_done", "rinv_done", "probs_done"))
        sum_done, clip_done, z_sum, ln_step, rstd_done, z_norm, z_scaled, resid_done = (sem(n) for n in (
            "sum_done", "clip_done", "z_sum", "ln_step", "rstd_done", "z_norm", "z_scaled", "resid_done"))
        L1_0, L2_0, HID_0, GELU_0, Z_0, Z_FREE_0 = 2, 2 * KT, 2, UNR, TT, 1

        def mm3(dst, w_hi, w_lo, a_hi, a_lo, start, stop, **kw):
            nc.tensor.matmul(dst, w_lo, a_hi, start=start, stop=False, **kw)
            nc.tensor.matmul(dst, w_hi, a_hi, start=False, stop=False, **kw)
            return nc.tensor.matmul(dst, w_hi, a_lo, start=False, stop=stop, **kw)

        def pe_transpose(src, bank0):
            for k in range(KT):
                for t in range(KT):
                    last = nc.tensor.transpose(ps[bank0 + k][:, t * P:(t + 1) * P],
                                               src[:, t, k * P:(k + 1) * P], ident[:, :])
                last.then_inc(tr_mm, 1)

        def pe_attention_1(pe, n, first):
            pe.wait_ge(x_in, 16 * (n + 1))
            if first:
                pe.wait_ge(fold_lo, KT)
            pe_transpose(x_raw, 4)
            if first:
                pe.wait_ge(fold_lo, 2 * KT)
            else:
                pe.wait_ge(proj_in, n * 64)
            for k in range(KT):
                pe.wait_ge(tr_lo, 12 + n * KT + k + 1)
                for j in range(KT):
                    if k == 0 and not first:
                        pe.wait_ge(sum_done, (n - 1) * KT + j + 1)
                    last = mm3(ps[j][:, :], aw_hi[:, 0, k * V + j * P:k * V + (j + 1) * P],
                               aw_lo[:, 0, k * V + j * P:k * V + (j + 1) * P],
                               x_hi[:, k, :], x_lo[:, k, :], k == 0, k == KT - 1)
                    if k == KT - 1:
                        last.then_inc(y_mm, 1)
            for t in range(TT):
                for k in range(KT):
                    last = mm3(ps[4 + t][:, :], x_hi[:, k, t * P:(t + 1) * P], x_lo[:, k, t * P:(t + 1) * P],
                               aw_hi[:, 1, k * V:(k + 1) * V], aw_lo[:, 1, k * V:(k + 1) * V],
                               k == 0, k == KT - 1)
                last.then_inc(v_mm, 1)
            pe.wait_ge(y_lo, n * KT + KT)
            for t in range(TT):
                seq = slice(t // TS * T, (t // TS + 1) * T)
                for k in range(KT):
                    last = mm3(ps[t][:, 0:T], ya_hi[:, k, t * P:(t + 1) * P], ya_lo[:, k, t * P:(t + 1) * P],
                               x_hi[:, k, seq], x_lo[:, k, seq], k == 0, k == KT - 1)
                last.then_inc(s_mm, 1)

        def pe_probs_T(pe, n, b):
            if b == 0:
                pe.wait_ge(v_lo, n * TT + TT)
            pe.wait_ge(probs_done, n * TT + (b + 1) * TS)
            for u in range(TS):
                for s in range(TS):
                    last = nc.tensor.transpose(ps[6 + b][:, u * T + s * P:u * T + (s + 1) * P],
                                               probs[:, b * TS + s, u * P:(u + 1) * P], ident[:, :])
            last.then_inc(pT_mm, 1)

        def pe_attend(pe, n):
            for b in range(SEQ):
                pe.wait_ge(pT_l, n * SEQ + b + 1)
                for e in range(KT):
                    for u in range(TS):
                        w = b * TS + u
                        last = mm3(ps[e][:, b * T:(b + 1) * T], vc_hi[:, w, e * P:(e + 1) * P],
                                   vc_lo[:, w, e * P:(e + 1) * P], pT_hi[:, b, u * T:(u + 1) * T],
                                   pT_lo[:, b, u * T:(u + 1) * T], u == 0, u == TS - 1)
                    if b == SEQ - 1:
                        last.then_inc(pv_mm, 1)

        def pe_down(pe, n, m, first_use):
            if m == 0:
                pe.wait_ge(e_lo, n * SEQ + SEQ)
                if first_use:
                    pe.wait_ge(v_lo, n * TT + 2 * TT)
            for b in range(SEQ):
                for k in range(KT):
                    if m == 0 and b == 0:
                        pe.wait_ge(xp_l, n * KT + k + 1)
                    w = slice(k * BN + m * P, k * BN + (m + 1) * P)
                    last = mm3(ps[4 + m][:, b * T:(b + 1) * T], aw_hi[:, b, w], aw_lo[:, b, w],
                               xp_hi[:, k, b * T:(b + 1) * T], xp_lo[:, k, b * T:(b + 1) * T],
                               k == 0, k == KT - 1)
            last.then_inc(down_mm, 1)

        def pe_up(pe, n):
            pe.wait_ge(h3_l, n * MT + MT)
            for t in range(TT):
                b, tok = t // TS, slice(t * P, (t + 1) * P)
                for m in range(MT):
                    w = slice(KT * BN + m * V, KT * BN + (m + 1) * V)
                    mm3(ps[4 + t][:, :], h3_hi[:, m, tok], h3_lo[:, m, tok], aw_hi[:, b, w], aw_lo[:, b, w],
                        m == 0, False)
                for k in range(KT):
                    dst = ps[4 + t][:, k * P:(k + 1) * P]
                    nc.tensor.matmul(dst, xp_hi[:, k, tok], ident_r[:, :], start=False, stop=False)
                    last = nc.tensor.matmul(dst, xp_lo[:, k, tok], ident_r[:, :], start=False, stop=k == KT - 1)
                last.then_inc(up_mm, 1)

        def pe_mlp(pe, n, phase):
            src = ((ya_hi, ya_lo, 0), (vc_hi, vc_lo, KT))

            def l1(q, g, part):
                a_hi, a_lo, k0 = src[part]
                for k in range(KT):
                    if part == 1:
                        pe.wait_ge(cms_lo, n * KT + k + 1)
                    last = mm3(ps[4 + q][:, :], w1_hi[:, q % 2, k0 + k, :], w1_lo[:, q % 2, k0 + k, :],
                               a_hi[:, k, :], a_lo[:, k, :], k0 + k == 0, part == phase and k == KT - 1)
                if part == phase:
                    last.then_inc(l1_mm, 1)

            def begin(q, g):
                pe.wait_ge(w1_l, g + 1)
                pe.wait_ge(gelu_done, g - UNR + 1 + GELU_0)
                if phase == 0:
                    pe.wait_ge(z_sum, n * TT + q % TT + 1)
                l1(q, g, 0)

            def l2(q, g, c):
                pe.wait_ge(w2_l, g + 1)
                pe.wait_ge(hid_l, g + 1 + HID_0)
                for j in range(KT):
                    w = slice(j * P, (j + 1) * P)
                    mm3(ps[j][:, :], w2_hi[:, q % 2, w], w2_lo[:, q % 2, w], hid_hi[:, q % 2, :],
                        hid_lo[:, q % 2, :], c, True, skip_group_check=True).then_inc(l2_mm, 1)

            def turn(g0, first):
                g = [g0 + q for q in range(UNR)]
                begin(0, g[0])
                begin(1, g[1])
                if phase:
                    l1(0, g[0], 1)
                    l1(1, g[1], 1)
                l2(0, g[0], first)
                for q in range(2, UNR):
                    begin(q, g[q])
                    if phase:
                        l1(q, g[q], 1)
                    l2(q - 1, g[q - 1], False)
                l2(UNR - 1, g[UNR - 1], False)

            base = n * CH + phase * NCH
            turn(base, True)
            with pe.Fori(1, ITS) as it:
                turn(base + it * UNR, False)

        def pe_program(pe):
            pe.sem_inc(l1_mm, L1_0)
            pe.sem_inc(l2_mm, L2_0)
            pe.wait_ge(ident_ready, 1)
            for t in range(KT):
                pe.wait_ge(fold_q[t], 16)
                for k in range(KT):
                    last = nc.tensor.transpose(ps[k][:, t * P:(t + 1) * P], x_raw[:, t, k * P:(k + 1) * P], ident[:, :])
                    if t == KT - 1:
                        last.then_inc(tr_mm, 1)
            pe.wait_ge(fold_in[1], 16)
            pe_transpose(wk_raw, 4)
            pe.wait_ge(fold_in[2], 16)
            pe.wait_ge(tr_lo, KT)
            pe_transpose(resid, 0)
            pe.wait_ge(tr_lo, 2 * KT)
            for m in range(KT):
                for k in range(KT):
                    last = mm3(ps[4 + m][:, :], ya_hi[:, k, m * P:(m + 1) * P], ya_lo[:, k, m * P:(m + 1) * P],
                               vc_hi[:, k, :], vc_lo[:, k, :], k == 0, k == KT - 1)
                last.then_inc(fold_mm, 1)
            pe.wait_ge(tr_lo, 3 * KT)
            pe.wait_ge(wp_l, 1)
            for m in range(KT):
                for k in range(KT):
                    last = mm3(ps[m][:, :], xp_hi[:, k, m * P:(m + 1) * P], xp_lo[:, k, m * P:(m + 1) * P],
                               x_hi[:, k, :], x_lo[:, k, :], k == 0, k == KT - 1)
                last.then_inc(fold_mm, 1)
            pe_attention_1(pe, 0, True)
            pe.wait_ge(v_lo, TT)
            pe.wait_ge(bias_in, 16 * len(BIAS))
            nc.tensor.transpose(ps[4][:, 0:NROW], bias_rows[0:NROW, :], ident[0:NROW, 0:NROW])
            pe.wait_ge(bd_in, 16 * B)
            for b in range(B):
                last = nc.tensor.transpose(ps[4][:, 64 + MT * b:64 + MT * (b + 1)],
                                           bd_rows[0:MT, b * P:(b + 1) * P], ident[0:MT, 0:MT])
            last.then_inc(bias_mm, 1)
            for b in range(SEQ):
                pe_probs_T(pe, 0, b)
            pe_attend(pe, 0)

            def mlps(n):
                pe.wait_ge(ao_lo, n * KT + KT)
                pe_mlp(pe, n, 0)
                pe_mlp(pe, n, 1)

            with pe.Fori(0, NB - 1) as n:
                mlps(n)
                pe_attention_1(pe, n + 1, False)
                for m in range(MT):
                    pe_down(pe, n, m, True)
                    pe_probs_T(pe, n + 1, m)
                pe_attend(pe, n + 1)
                pe_up(pe, n)
            mlps(NB - 1)
            for m in range(MT):
                pe_down(pe, NB - 1, m, False)
            pe_up(pe, NB - 1)

        def slot_views(phase, s):
            k = KIN[phase]
            return w1_hi[:, s, 0:k, :], w1_lo[:, s, 0:k, :], w1_raw[:, s, 0:k, :]

        def act_w1(act, phase, q, g, pair):
            act.wait_ge(w1_in[q % 2], 16 * pair + 16)
            act.wait_ge(l1_mm, g - 2 + 1 + L1_0)
            hi, _, raw = slot_views(phase, q % 2)
            nc.scalar.activation(hi, raw, ACT.Copy).then_inc(w1_h, 1)

        def act_w2(act, q, g, pair):
            act.wait_ge(w2_in[q % 2], 16 * pair + 16)
            act.wait_ge(l2_mm, (g - 2 + 1) * KT + L2_0)
            nc.scalar.activation(w2_hi[:, q % 2, :], w2_raw[:, q % 2, :], ACT.Copy).then_inc(w2_h, 1)

        def act_gelu(act, phase, q, g, col):
            act.wait_ge(l1_mm, g + 1 + L1_0)
            act.wait_ge(l2_mm, (g - 2 + 1) * KT + L2_0)
            act.wait_ge(hid_l, g - 2 + 1 + HID_0)
            b = bias[:, bass.ds(MLP_B[phase] + col, 1)] if not isinstance(col, int) else \
                bias[:, MLP_B[phase] + col:MLP_B[phase] + col + 1]
            nc.scalar.activation(hid_hi[:, q % 2, :], ps[4 + q][:, :], ACT.Gelu, bias=b)
            nc.scalar.activation(gel[:, q % 2, :], ps[4 + q][:, :], ACT.Gelu, bias=b).then_inc(gelu_done, 1)

        def chunk_steps(phase, n, it, last, w1, w2, gelu):
            q0 = phase * NCH
            g0 = n * CH + q0 + it * UNR
            h0 = n * NCH + (q0 + it * UNR) // 2 if isinstance(it, int) else n * NCH + q0 // 2 + it * (UNR // 2)
            nxt = 1 if last and phase == 0 else (0 if last else phase)
            w1n = lambda q: w1(nxt if q >= UNR else phase, q % UNR, g0 + q, h0 + q // 2)
            w2n = lambda q: w2(q % UNR, g0 + q, h0 + q // 2)
            more = not (last and phase == 1 and isinstance(n, int))
            col = it * UNR
            gelu(phase, 0, g0, col)
            w1n(2)
            gelu(phase, 1, g0 + 1, col + 1)
            w1n(3)
            w2n(2)
            gelu(phase, 2, g0 + 2, col + 2)
            w2n(3)
            if more:
                w1n(4)
            gelu(phase, 3, g0 + 3, col + 3)
            if more:
                w2n(4)
                w1n(5)
                if not last:
                    w2n(5)

        def act_tiles(act, mm, n0, banks, hi, sem_out, func=ACT.Copy, width=512, **kw):
            for k, bank in enumerate(banks):
                act.wait_ge(mm, n0 + k + 1)
                nc.scalar.activation(hi[:, k, :], ps[bank][:, :], func,
                                     **{a: f(k) for a, f in kw.items()}).then_inc(sem_out, 1)

        def act_attention_1(act, n, first):
            if not first:
                act.wait_ge(resid_done, n * 3)
            act_tiles(act, tr_mm, 12 + n * KT, range(4, 8), x_hi, tr_hi)
            act_tiles(act, y_mm, n * KT, range(4), ya_hi, y_hi)

        def act_softmax(act, n):
            act_tiles(act, v_mm, n * KT, range(4, 8), vc_hi, v_hi)

        def act_exps(act, n):
            if not isinstance(n, int):
                act.wait_ge(z_free, n)
            for t in range(TT):
                act.wait_ge(nmax_done, n * TT + t + 1)
                nc.scalar.activation(probs[:, t, :], ps[t][:, 0:T], ACT.Exp, bias=nmx[:, t:t + 1], scale=SCALE,
                                     accum_out=rsum[:, t:t + 1]).then_inc(exp_done, 1)

        def act_probs_T(act, n):
            for b in range(SEQ):
                act.wait_ge(pT_mm, n * SEQ + b + 1)
                nc.scalar.activation(pT_hi[:, b, :], ps[6 + b][:, :], ACT.Copy).then_inc(pT_h, 1)

        def act_attention(act, n):
            act_tiles(act, pv_mm, n * KT, range(4), ya_hi, ao_hi, ACT.Identity,
                      bias=lambda k: bias[:, BP + k:BP + k + 1])

        def act_expert_weights(act, n, b):
            act.wait_ge((e_in, e1_in)[b], 32 * n + 32)
            nc.scalar.activation(aw_hi[:, b, :], e_raw[:, :, :].rearrange("p a n -> p (a n)"), ACT.Copy)\
                .then_inc(e_hi, 1)

        def act_down(act, n):
            for m in range(MT):
                act.wait_ge(down_mm, n * MT + m + 1)
                for b in range(SEQ):
                    col, cols = bd_cur[:, b * MT + m:b * MT + m + 1], slice(b * T, (b + 1) * T)
                    nc.scalar.activation(h3_hi[:, m, cols], ps[4 + m][:, cols], ACT.Gelu, bias=col)
                    last = nc.scalar.activation(gel[:, m, cols], ps[4 + m][:, cols], ACT.Gelu, bias=col)
                last.then_inc(h3_h, 1)

        def act_xp(act, n):
            for j in range(KT):
                act.wait_ge(clip_done, n * KT + j + 1)
                nc.scalar.activation(xp_hi[:, j, :], resid[:, j, :], ACT.Copy).then_inc(xp_h, 1)

        def act_program(act):
            act.sem_inc(gelu_done, GELU_0)
            at = 0
            for (src, n), off in zip(BIAS, offs):
                act.dma_start(bias_rows[off:off + n // P, :], src.rearrange("(r p) -> r p", p=P)).then_inc(bias_in, 16)
            act_tiles(act, tr_mm, 0, range(4), ya_hi, tr_hi)
            act_tiles(act, tr_mm, KT, range(4, 8), vc_hi, tr_hi)
            act_tiles(act, tr_mm, 2 * KT, range(4), xp_hi, tr_hi)
            act.wait_ge(fold_in[3], 16)
            nc.scalar.activation(x_hi[:, :, :], wp_raw, ACT.Copy).then_inc(wp_h, 1)
            for slot, banks in ((0, range(4, 8)), (1, range(4))):
                for m, bank in enumerate(banks):
                    act.wait_ge(fold_mm, slot * KT + m + 1)
                    nc.scalar.activation(aw_hi[:, slot, m * V:(m + 1) * V], ps[bank][:, :], ACT.Copy)\
                        .then_inc(fold_hi, 1)
            act_attention_1(act, 0, True)
            act_w1(act, 0, 0, 0, 0)
            act_w2(act, 0, 0, 0)
            act_softmax(act, 0)
            act_w1(act, 0, 1, 1, 0)
            act_w2(act, 1, 1, 0)
            act_exps(act, 0)
            act_probs_T(act, 0)
            act.wait_ge(bias_ready, 2)
            nc.scalar.activation(warm[:, :], bias[:, 0:1], ACT.Gelu)
            act_attention(act, 0)

            def mlps(n):
                for phase in range(2):
                    steps = lambda it, last: chunk_steps(
                        phase, n, it, last, lambda ph, q, g, h: act_w1(act, ph, q, g, h),
                        lambda q, g, h: act_w2(act, q, g, h), lambda ph, q, g, c: act_gelu(act, ph, q, g, c))
                    if phase == 1 and isinstance(n, int):
                        with act.Fori(0, ITS - 2) as it:
                            steps(it, False)
                        act_expert_weights(act, n, 0)
                        steps(ITS - 2, False)
                        act_expert_weights(act, n, 1)
                    else:
                        with act.Fori(0, ITS - 1) as it:
                            steps(it, False)
                    steps(ITS - 1, True)
                    if phase == 0:
                        act.wait_ge(cur_bias, n * 2 + 2)
                        for j in range(KT):
                            act.wait_ge(l2_mm, (n * CH + NCH - 1) * KT + j + 1 + L2_0)
                            for b in range(SEQ):
                                cols = slice(b * T, (b + 1) * T)
                                last = nc.scalar.activation(vc_hi[:, j, cols], ps[j][:, cols], ACT.Identity,
                                                            bias=cb_cur[:, j, b:b + 1])
                            last.then_inc(cms_hi, 1)
                        act_w2(act, 1, n * CH + NCH + 1, n * NCH + NCH // 2)

            with act.Fori(0, NB - 1) as n:
                mlps(n)
                act_attention_1(act, n + 1, False)
                act_w2(act, 1, n * CH + CH + 1, n * NCH + NCH)
                act_expert_weights(act, n, 0)
                act_xp(act, n)
                act_softmax(act, n + 1)
                act_expert_weights(act, n, 1)
                act_exps(act, n + 1)
                act_probs_T(act, n + 1)
                act_down(act, n)
                act_attention(act, n + 1)
            mlps(NB - 1)
            act_xp(act, NB - 1)
            act_down(act, NB - 1)

        sub = lambda dst, a, hi: nc.vector.tensor_tensor(dst, a, hi.bitcast(F32), ALU.subtract)

        def dve_w1(dve, phase, q, g, pair):
            dve.wait_ge(w1_h, g + 1)
            hi, lo, raw = slot_views(phase, q % 2)
            sub(lo, raw, hi).then_inc(w1_l, 1)

        def dve_w2(dve, q, g, pair):
            dve.wait_ge(w2_h, g + 1)
            sub(w2_lo[:, q % 2, :], w2_raw[:, q % 2, :], w2_hi[:, q % 2, :]).then_inc(w2_l, 1)

        def dve_gelu(dve, phase, q, g, col):
            dve.wait_ge(gelu_done, g + 1 + GELU_0)
            sub(hid_lo[:, q % 2, :], gel[:, q % 2, :], hid_hi[:, q % 2, :]).then_inc(hid_l, 1)

        def dve_tiles(dve, hi_sem, n0, banks, hi, lo, lo_sem):
            for k, bank in enumerate(banks):
                dve.wait_ge(hi_sem, n0 + k + 1)
                sub(lo[:, k, :], ps[bank][:, :], hi[:, k, :]).then_inc(lo_sem, 1)

        def dve_y(dve, n):
            dve_tiles(dve, y_hi, n * KT, range(4), ya_hi, ya_lo, y_lo)

        def dve_v(dve, n):
            dve_tiles(dve, v_hi, n * KT, range(4, 8), vc_hi, vc_lo, v_lo)

        def dve_softmax(dve, n):
            def row_max(t):
                dve.wait_ge(s_mm, n * TT + t + 1)
                nc.vector.reduce_max(mx[:, t:t + 1], ps[t][:, 0:T], AX_X).then_inc(max_done, 1)

            def shift(t):
                dve.wait_ge(max_done, n * TT + t + 1)
                nc.vector.tensor_scalar_mul(nmx[:, t:t + 1], mx[:, t:t + 1], -SCALE).then_inc(nmax_done, 1)

            row_max(0)
            for t in range(1, TT):
                row_max(t)
                shift(t - 1)
            shift(TT - 1)

        def dve_probs(dve, n):
            for t in range(TT):
                dve.wait_ge(exp_done, n * TT + t + 1)
                nc.vector.reciprocal(rinv[:, t:t + 1], rsum[:, t:t + 1]).then_inc(rinv_done, 1)
                dve.wait_ge(rinv_done, n * TT + t + 1)
                nc.vector.tensor_scalar_mul(probs[:, t, :], probs[:, t, :], rinv[:, t:t + 1])\
                    .then_inc(probs_done, 1)

        def dve_probs_T(dve, n):
            for b in range(SEQ):
                dve.wait_ge(pT_h, n * SEQ + b + 1)
                sub(pT_lo[:, b, :], ps[6 + b][:, :], pT_hi[:, b, :]).then_inc(pT_l, 1)

        def dve_attention(dve, n):
            for e in range(KT):
                dve.wait_ge(ao_hi, n * KT + e + 1)
                nc.vector.scalar_tensor_tensor(out=ya_lo[:, e, :], in0=ps[e][:, :], scalar=bias[:, BP + e:BP + e + 1],
                                               in1=ya_hi[:, e, :].bitcast(F32), op0=ALU.add, op1=ALU.subtract)\
                    .then_inc(ao_lo, 1)

        def dve_expert_weights(dve, n, b):
            dve.wait_ge(e_hi, n * SEQ + b + 1)
            sub(aw_lo[:, b, :], e_raw[:, :, :].rearrange("p a n -> p (a n)"), aw_hi[:, b, :]).then_inc(e_lo, 1)

        def dve_sum(dve, n, j):
            if j == 0:
                dve.wait_ge(resid_done, n * 3 + 3)
            dve.wait_ge(l2_mm, (n * CH + CH - 1) * KT + j + 1 + L2_0)
            nc.vector.scalar_tensor_tensor(out=resid[:, j, :], in0=ps[j][:, :], scalar=bias[:, MB2 + j:MB2 + j + 1],
                                           in1=resid[:, j, :], op0=ALU.add, op1=ALU.add).then_inc(sum_done, 1)

        def dve_clip(dve, n, j):
            dve.wait_ge(sum_done, n * KT + j + 1)
            nc.vector.tensor_scalar(resid[:, j, :], resid[:, j, :], 0.0, 1.0, ALU.max, ALU.min).then_inc(clip_done, 1)

        def dve_xp(dve, n, j):
            dve.wait_ge(xp_h, n * KT + j + 1)
            sub(xp_lo[:, j, :], resid[:, j, :], xp_hi[:, j, :]).then_inc(xp_l, 1)

        def dve_x_lo(dve, n, k):
            dve.wait_ge(tr_hi, 12 + n * KT + k + 1)
            sub(x_lo[:, k, :], ps[4 + k][:, :], x_hi[:, k, :]).then_inc(tr_lo, 1)

        def dve_h3(dve, n):
            for m in range(MT):
                dve.wait_ge(h3_h, n * MT + m + 1)
                sub(h3_lo[:, m, :], gel[:, m, :], h3_hi[:, m, :]).then_inc(h3_l, 1)

        def dve_layer_norm(dve, n, last):
            def stats(t):
                dve.wait_ge(up_mm, n * TT + t + 1)
                if t == 0:
                    dve.wait_ge(ln_in, 16 * 3 * SEQ * (n + 1))
                dve.wait_ge(z_free, n + Z_FREE_0)
                nc.vector.tensor_tensor(z[t], ps[4 + t][:, :], ln_p[:, t // TS, 0, :], ALU.add).then_inc(z_sum, 1)
                s = n * 3 * TT + 3 * t
                dve.wait_ge(z_sum, n * TT + t + 1 + Z_0)
                nc.vector.bn_stats(stat[:, t, :], z[t]).then_inc(ln_step, 1)
                dve.drain()
                nc.vector.bn_aggr(mv[:, t, :], stat[:, t, :]).then_inc(ln_step, 1)
                dve.wait_ge(ln_step, s + 2)
                nc.vector.tensor_scalar_add(veps[:, t:t + 1], mv[:, t, 1:2], LN_EPS).then_inc(ln_step, 1)

            def norm(t):
                dve.wait_ge(rstd_done, n * TT + t + 1)
                nc.vector.tensor_scalar(z[t], z[t], mv[:, t, 0:1], rstd[:, t:t + 1], ALU.subtract, ALU.mult)\
                    .then_inc(z_norm, 1)
                if last:
                    dve.wait_ge(z_norm, n * TT + t + 1)
                    nc.vector.tensor_tensor(z[t], z[t], ln_p[:, t // TS, 1, :], ALU.mult).then_inc(last_step, 1)
                    dve.wait_ge(last_step, t + 1)
                    nc.vector.tensor_tensor(z[t], z[t], ln_p[:, t // TS, 2, :], ALU.add).then_inc(z_last, 1)

            stats(0)
            for t in range(1, TT):
                stats(t)
                norm(t - 1)
            norm(TT - 1)

        def dve_columns(n):
            nc.vector.tensor_copy(bd_cur[:, :], bd_all[:, bass.ds(n * (SEQ * MT), SEQ * MT)]).then_inc(cur_bias, 1)
            flat = cb_all[:, :, :, :].rearrange("p n k s -> p (n k s)")
            nc.vector.tensor_copy(cb_cur[:, :, :].rearrange("p k s -> p (k s)"),
                                  flat[:, bass.ds(n * (KT * SEQ), KT * SEQ)]).then_inc(cur_bias, 1)

        def dve_program(dve):
            dve.sem_inc(hid_l, HID_0)
            dve.sem_inc(z_sum, Z_0)
            nc.vector.memset(mhalf[:, :], -0.5).then_inc(consts, 1)
            dve.wait_ge(experts_in, 16)
            nc.vector.tensor_scalar(exp_n[:, :], exp_i[:, :], 0.0, float(E), ALU.is_lt, ALU.mult).then_inc(ids_step, 1)
            dve.wait_ge(ids_step, 1)
            nc.vector.tensor_tensor(exp_f[:, :], exp_n[:, :], exp_i[:, :], ALU.add).then_inc(ids_step, 1)
            dve.wait_ge(ids_step, 2)
            nc.vector.tensor_scalar(exp_id[:, :], exp_f[:, :], 0.0, float(E - 1), ALU.max, ALU.min)\
                .then_inc(ids_ready, 1)
            dve.wait_ge(ident_ready, 1)
            nc.vector.tensor_copy(ident_r[:, :], ident[:, :]).then_inc(consts, 1)
            dve_tiles(dve, tr_hi, 0, range(4), ya_hi, ya_lo, tr_lo)
            dve_tiles(dve, tr_hi, KT, range(4, 8), vc_hi, vc_lo, tr_lo)
            dve_tiles(dve, tr_hi, 2 * KT, range(4), xp_hi, xp_lo, tr_lo)
            dve.wait_ge(wp_h, 1)
            sub(x_lo[:, :, :], wp_raw, x_hi[:, :, :]).then_inc(wp_l, 1)
            for slot, banks in ((0, range(4, 8)), (1, range(4))):
                for m, bank in enumerate(banks):
                    dve.wait_ge(fold_hi, slot * KT + m + 1)
                    cols = slice(m * V, (m + 1) * V)
                    sub(aw_lo[:, slot, cols], ps[bank][:, :], aw_hi[:, slot, cols]).then_inc(fold_lo, 1)
            for k in range(KT):
                dve_x_lo(dve, 0, k)
            dve_y(dve, 0)
            dve_w1(dve, 0, 0, 0, 0)
            dve_w2(dve, 0, 0, 0)
            dve_v(dve, 0)
            dve_w1(dve, 0, 1, 1, 0)
            dve_w2(dve, 1, 1, 0)
            dve_softmax(dve, 0)
            dve_probs(dve, 0)
            dve.wait_ge(bias_mm, 1)
            nc.vector.tensor_copy(bias[:, :], ps[4][:, 0:NROW]).then_inc(bias_ready, 1)
            nc.vector.tensor_copy(bd_all[:, :], ps[4][:, 64:64 + B * MT]).then_inc(bias_ready, 1)
            dve.wait_ge(codes_in, 16)
            dve.wait_ge(iotas, 1)
            nc.vector.tensor_copy(codes_f[:, :], codes_i[:, :]).then_inc(cb_step, 1)
            nc.vector.tensor_copy(feat_f[:, :], feat_i[:, :]).then_inc(cb_step, 1)
            dve.wait_ge(cb_step, 2)
            dve.wait_ge(bias_ready, 2)
            for k in range(KT):
                nc.vector.tensor_scalar(cb_all[:, :, k, :], codes_f[:, :].rearrange("p (n s) -> p n s", s=SEQ),
                                        feat_f[:, k:k + 1], bias[:, CB2 + k:CB2 + k + 1], ALU.is_equal, ALU.add)\
                    .then_inc(cb_step, 1)
            dve.wait_ge(cb_step, 2 + KT)
            dve_probs_T(dve, 0)
            dve_attention(dve, 0)

            def mlps(n):
                dve_columns(n)
                for phase in range(2):
                    steps = lambda it, last: chunk_steps(
                        phase, n, it, last, lambda ph, q, g, h: dve_w1(dve, ph, q, g, h),
                        lambda q, g, h: dve_w2(dve, q, g, h), lambda ph, q, g, c: dve_gelu(dve, ph, q, g, c))
                    if phase == 1 and isinstance(n, int):
                        with dve.Fori(0, ITS - 2) as it:
                            steps(it, False)
                        dve_expert_weights(dve, n, 0)
                        steps(ITS - 2, False)
                        dve_expert_weights(dve, n, 1)
                    else:
                        with dve.Fori(0, ITS - 1) as it:
                            steps(it, False)
                    steps(ITS - 1, True)
                    if phase == 0:
                        dve.wait_ge(cur_bias, n * 2 + 2)
                        for j in range(KT):
                            dve.wait_ge(cms_hi, n * KT + j + 1)
                            for b in range(SEQ):
                                cols = slice(b * T, (b + 1) * T)
                                last = nc.vector.scalar_tensor_tensor(
                                    out=vc_lo[:, j, cols], in0=ps[j][:, cols], scalar=cb_cur[:, j, b:b + 1],
                                    in1=vc_hi[:, j, cols].bitcast(F32), op0=ALU.add, op1=ALU.subtract)
                            last.then_inc(cms_lo, 1)
                        dve_w2(dve, 1, n * CH + NCH + 1, 0)

            with dve.Fori(0, NB - 1) as n:
                mlps(n)
                for j in range(KT):
                    dve_sum(dve, n, j)
                    if j >= 2:
                        dve_x_lo(dve, n + 1, j - 2)
                dve_x_lo(dve, n + 1, 2)
                dve_x_lo(dve, n + 1, 3)
                for j in range(KT):
                    dve_clip(dve, n, j)
                dve_y(dve, n + 1)
                dve_w2(dve, 1, n * CH + CH + 1, 0)
                dve_expert_weights(dve, n, 0)
                for j in range(KT):
                    dve_xp(dve, n, j)
                dve_v(dve, n + 1)
                dve_expert_weights(dve, n, 1)
                dve_softmax(dve, n + 1)
                dve_probs(dve, n + 1)
                dve_probs_T(dve, n + 1)
                dve_h3(dve, n)
                dve_attention(dve, n + 1)
                dve_layer_norm(dve, n, False)
            mlps(NB - 1)
            for j in range(KT + 2):
                if j < KT:
                    dve_sum(dve, NB - 1, j)
                if 1 <= j <= KT:
                    dve_clip(dve, NB - 1, j - 1)
                if j >= 2:
                    dve_xp(dve, NB - 1, j - 2)
            dve_h3(dve, NB - 1)
            dve_layer_norm(dve, NB - 1, True)

        def pool_residual(pool, n):
            pool.wait_ge(cms_lo, n * KT + KT)
            nc.gpsimd.tensor_tensor(resid[:, :, :], vc_hi[:, :, :].bitcast(F32), vc_lo[:, :, :].bitcast(F32),
                                    ALU.add).then_inc(resid_done, 1)
            pool.wait_ge(resid_done, n * 3 + 1)
            nc.gpsimd.tensor_tensor(resid[:, :, :], resid[:, :, :], x_hi[:, :, :].bitcast(F32), ALU.add)\
                .then_inc(resid_done, 1)
            pool.wait_ge(resid_done, n * 3 + 2)
            nc.gpsimd.tensor_tensor(resid[:, :, :], resid[:, :, :], x_lo[:, :, :].bitcast(F32), ALU.add)\
                .then_inc(resid_done, 1)

        def load_expert(eng, n, b, landed):
            e = eng.value_load(exp_id[0:1, bass.ds(n * SEQ + b, 1)], min_val=0, max_val=E - 1)
            eng.dma_start(e_raw[:, 0, :].rearrange("p (k n) -> p k n", k=KT),
                          down_v[:, bass.ds(e * KT, KT), :]).then_inc(landed, 16)
            eng.dma_start(e_raw[:, 1, :].rearrange("p (k n) -> p k n", k=MT),
                          up_v[:, bass.ds(e * MT, MT), :]).then_inc(landed, 16)

        def pool_expert(pool, n, last):
            pool.wait_ge(e_lo, n * SEQ + 1)
            load_expert(pool, n, 1, e1_in)

            def power(t):
                pool.wait_ge(ln_step, n * 3 * TT + 3 * t + 3)
                nc.gpsimd.tensor_tensor(rstd[:, t:t + 1], veps[:, t:t + 1], mhalf[:, :], ALU.pow)\
                    .then_inc(rstd_done, 1)

            def scale_and_store(t):
                s = n * 2 * TT + 2 * t
                pool.wait_ge(z_norm, n * TT + t + 1)
                nc.gpsimd.tensor_tensor(z[t], z[t], ln_p[:, t // TS, 1, :], ALU.mult).then_inc(z_scaled, 1)
                pool.wait_ge(z_scaled, s + 1)
                nc.gpsimd.tensor_tensor(z[t], z[t], ln_p[:, t // TS, 2, :], ALU.add).then_inc(z_scaled, 1)
                pool.wait_ge(z_scaled, s + 2)
                pool.dma_start(out_rows[bass.ds(n * TB + t * P, P), :], z[t]).then_inc(stored[t], 16)

            for t in range(TT):
                power(t)
            if last:
                return
            for t in range(TT):
                scale_and_store(t)
            for t in range(TT):
                pool.wait_ge(stored[t], 16 * n + 16)
            pool.sem_inc(z_free, 1)

        def pool_program(pool):
            pool.sem_inc(z_free, Z_FREE_0)
            nc.gpsimd.memset(ident[:, :], 0.0).then_inc(iotas, 1)
            nc.gpsimd.iota(feat_i[:, :], pattern=[[P, KT]], base=0, channel_multiplier=1).then_inc(iotas, 1)
            pool.wait_ge(iotas, 2)
            nc.gpsimd.affine_select(out=ident[:, :], in_=ident[:, :], compare_op=ALU.not_equal, fill=1.0, base=0,
                                    pattern=[[-1, P]], channel_multiplier=1).then_inc(ident_ready, 1)
            pool.wait_ge(ids_ready, 1)
            with pool.Fori(0, B) as b:
                e = pool.value_load(exp_id[0:1, bass.ds(b, 1)], min_val=0, max_val=E - 1)
                pool.dma_start(bd_rows[:, bass.ds(b * P, P)], bdown_v[bass.ds(e * MT, MT), :]).then_inc(bd_in, 16)
            pool.wait_ge(consts, 1)
            with pool.Fori(0, NB - 1) as n:
                pool_residual(pool, n)
                pool_expert(pool, n, False)
            pool_residual(pool, NB - 1)
            pool_expert(pool, NB - 1, True)

        def load_chunk(sp, phase, s, g, c):
            k = KIN[phase]
            sp.dma_start(w1_raw[:, s, 0:k, :], mlp_w1[phase][:, :, bass.ds(c, P)]).then_inc(w1_in[s], 16)
            sp.dma_start(w2_raw[:, s, :], mlp_w2[phase][bass.ds(c, P), :]).then_inc(w2_in[s], 16)

        def turn_loads(sp, n, more):
            def tokens():
                sp.wait_ge(tr_mm, 12 + n * KT + KT)
                sp.dma_start(x_raw[:, :, :], x_rows[bass.ds((n + 1) * TB, TB), :]
                             .rearrange("(t p) v -> p t v", p=P)).then_inc(x_in, 16)

            def projection(slot):
                sp.wait_ge(v_mm, n * TT + TT)
                sp.dma_start(aw_hi[:, slot, :].bitcast(F32), proj_hi[:, slot, :]).then_inc(proj_in, 16)
                sp.dma_start(aw_lo[:, slot, :].bitcast(F32), proj_lo[:, slot, :]).then_inc(proj_in, 16)

            def norm_rows(b):
                e = sp.value_load(exp_id[0:1, bass.ds(n * SEQ + b, 1)], min_val=0, max_val=E - 1)
                for i, src in enumerate(ln_v):
                    sp.dma_start(ln_p[:, b, i, :], src[bass.ds(e, 1), :].to_broadcast([P, V])).then_inc(ln_in, 16)

            own = [lambda: load_expert(sp, n, 0, e_in), lambda: norm_rows(0), lambda: norm_rows(1)]
            return own + [tokens, lambda: projection(0), lambda: projection(1)] if more else own

        def sync_program(sp):
            sp.dma_start(exp_i[:, :], row_of(experts)).then_inc(experts_in, 16)
            for t in range(KT):
                sp.dma_start(x_raw[:, t, :], square[0][:, t, :]).then_inc(fold_q[t], 16)
            sp.dma_start(wk_raw, square[1]).then_inc(fold_in[1], 16)
            sp.dma_start(codes_i[:, :], row_of(codes).to_broadcast([P, B])).then_inc(codes_in, 16)
            sp.dma_start(resid[:, :, :], square[2]).then_inc(fold_in[2], 16)
            sp.dma_start(wp_raw, square[3]).then_inc(fold_in[3], 16)
            sp.wait_ge(tr_mm, KT)
            sp.dma_start(x_raw[:, :, :], x_rows[0:TB, :].rearrange("(t p) v -> p t v", p=P)).then_inc(x_in, 16)
            sp.wait_ge(wp_l, 1)
            load_chunk(sp, 0, 0, 0, 0)
            load_chunk(sp, 0, 1, 1, P)
            sp.wait_ge(fold_lo, 2 * KT)
            for slot in range(2):
                sp.dma_start(proj_hi[:, slot, :], aw_hi[:, slot, :].bitcast(F32)).then_inc(proj_out, 16)
                sp.dma_start(proj_lo[:, slot, :], aw_lo[:, slot, :].bitcast(F32)).then_inc(proj_out, 16)
            sp.wait_ge(ids_ready, 1)
            sp.wait_ge(proj_out, 64)

            def chunk_pair(phase, g, c):
                for s in range(2):
                    sp.wait_ge(w1_l, g + s - 1)
                    sp.wait_ge(w2_l, g + s - 1)
                    load_chunk(sp, phase, s, g + s, c + s * P)

            def mlps(n, more):
                with sp.Fori(1, NCH // 2) as j:
                    chunk_pair(0, n * CH + j * 2, j * (2 * P))
                sp.wait_ge(z_free, n + Z_FREE_0)
                pieces = turn_loads(sp, n, more)
                for j in range(NCH // 2):
                    chunk_pair(1, n * CH + NCH + j * 2, j * (2 * P))
                    if j < len(pieces):
                        pieces[j]()
                if more:
                    chunk_pair(0, n * CH + CH, 0)

            with sp.Fori(0, NB - 1) as n:
                mlps(n, True)
            mlps(NB - 1, False)
            for t in range(TT):
                sp.wait_ge(z_last, t + 1)
                sp.dma_start(out_rows[(NB - 1) * TB + t * P:(NB - 1) * TB + (t + 1) * P, :], z[t])\
                    .then_inc(stored_last, 16)
            sp.wait_ge(stored_last, 16 * TT)

        block = ctx.enter_context(nc.Block())

        @block.sync
        def _(sp):
            sync_program(sp)

        @block.gpsimd
        def _(pool):
            pool_program(pool)

        @block.scalar
        def _(act):
            act_program(act)

        @block.vector
        def _(dve):
            dve_program(dve)

        @block.tensor
        def _(pe):
            pe_program(pe)


_INS = ['x', 'itok_B_17_1546', 'itok_B_1_2', 'L0_cond_Wq', 'L0_cond_Wk', 'L0_cond_Wv', 'L0_cond_Wp', 'L0_cond_bp',
        'L0_cond_cW1', 'L0_cond_cb1', 'L0_cond_cW2', 'L0_cond_cb2', 'L0_cond_mW1', 'L0_cond_mb1', 'L0_cond_mW2',
        'L0_cond_mb2', 'L1_cond_W_down', 'L1_cond_b_down', 'L1_cond_W_up', 'L1_cond_b_up', 'L1_cond_ln_w',
        'L1_cond_ln_b']


def kernel(**inputs):
    import numpy as np
    import concourse.bacc as bacc
    from concourse.bass_utils import run_bass_kernel_spmd as run

    nc = bacc.Bacc("TRN2", target_bir_lowering=False, num_devices=1)
    arrays, args = {}, []
    for name in _INS:
        a = np.ascontiguousarray(inputs[name])
        arrays[f"in_{name}"] = a
        args.append(nc.dram_tensor(f"in_{name}", a.shape, mybir.dt.from_np(a.dtype), kind="ExternalInput").ap())
    shape = inputs['x'].shape
    args.append(nc.dram_tensor("out_0", shape, F32, kind="ExternalOutput").ap())
    build(nc, *args)
    r = run(nc, [arrays], core_ids=[0])
    return r.results[0]["out_0"]
```

```python
from contextlib import ExitStack

import concourse.bass as bass
from concourse import mybir

F32 = mybir.dt.float32
F32R = mybir.dt.float32r
I32 = mybir.dt.int32
ACT = mybir.ActivationFunctionType
ALU = mybir.AluOpType
AX_X = mybir.AxisListType.X

P = 128
LN_EPS = 1e-5


def build(nc, x, codes, experts, Wq, Wk, Wv, Wp, bp, cW1, cb1, cW2, cb2, mW1, mb1, mW2, mb2,
          W_down, b_down, W_up, b_up, ln_w, ln_b, out):
    B, T, V = x.shape
    H = cW1.shape[1]
    E, _, BN = W_down.shape
    SEQ = 2
    TB = SEQ * T
    NB = B // SEQ
    KT = V // P
    TT = TB // P
    TS = T // P
    MT = BN // P
    NCH = H // P
    CH = 2 * NCH
    UNR = 4
    ITS = NCH // UNR
    UP_ORDER = (2, 3, 0, 1)
    LAST_DOWN = ((1, 0), (1, 1), (0, 0), (0, 1))
    SCALE = float(V) ** -0.5
    KIN = (KT, 2 * KT)

    x_rows = x.rearrange("b t v -> (b t) v")
    out_rows = out.rearrange("b t v -> (b t) v")
    mlp_w1 = (cW1.rearrange("(k p) n -> p k n", p=P), mW1.rearrange("(k p) n -> p k n", p=P))
    mlp_w2 = (cW2, mW2)
    square = [w.rearrange("(k p) n -> p k n", p=P) for w in (Wq, Wk, Wv, Wp)]
    down_v = W_down.rearrange("e (k p) n -> p (e k) n", p=P)
    up_v = W_up.rearrange("e (k p) n -> p (e k) n", p=P)
    bdown_v = b_down.rearrange("e (m p) -> (e m) p", p=P)
    row_of = lambda a: a.rearrange("(o b) -> o b", o=1)
    ln_v = (b_up, ln_w, ln_b)
    proj_hi = nc.dram_tensor("proj_hi", (P, 2, KT * V), F32, kind="Internal").ap()
    proj_lo = nc.dram_tensor("proj_lo", (P, 2, KT * V), F32, kind="Internal").ap()

    BIAS = ((bp, V), (cb1, H), (cb2, V), (mb1, H), (mb2, V))
    at, offs = 0, []
    for _, n in BIAS:
        offs.append(at)
        at += n // P
    NROW = at
    BP, CB1, CB2, MB1, MB2 = offs
    MLP_B = (CB1, MB1)

    with ExitStack() as ctx:
        sb = lambda name, shape, dt=F32: ctx.enter_context(nc.sbuf_tensor(name, shape, dt))
        sem = lambda name: ctx.enter_context(nc.semaphore(name))

        ident = sb("ident", [P, P])
        x_raw = sb("x_raw", [P, TT, V])
        e_raw = sb("e_raw", [P, 2, KT * BN])
        w1_raw = sb("w1_raw", [P, 2, 2 * KT, P])
        w2_raw = sb("w2_raw", [P, 2, V])
        w1_hi, w1_lo = (sb(n, [P, 2, 2 * KT, P], F32R) for n in ("w1_hi", "w1_lo"))
        w2_hi, w2_lo = (sb(n, [P, 2, V], F32R) for n in ("w2_hi", "w2_lo"))
        aw_hi, aw_lo = (sb(n, [P, 2, KT * V], F32R) for n in ("aw_hi", "aw_lo"))
        x_hi, x_lo = (sb(n, [P, KT, TB], F32R) for n in ("x_hi", "x_lo"))
        ya_hi, ya_lo = (sb(n, [P, KT, TB], F32R) for n in ("ya_hi", "ya_lo"))
        vc_hi, vc_lo = (sb(n, [P, KT, TB], F32R) for n in ("vc_hi", "vc_lo"))
        xp_hi, xp_lo = (sb(n, [P, KT, TB], F32R) for n in ("xp_hi", "xp_lo"))
        resid = sb("resid", [P, KT, TB])
        probs = sb("probs", [P, TT, T])
        pT_hi, pT_lo = (sb(n, [P, SEQ, TS * T], F32R) for n in ("pT_hi", "pT_lo"))
        h3_hi, h3_lo = (sb(n, [P, MT, TB], F32R) for n in ("h3_hi", "h3_lo"))
        gel = sb("gel", [P, 2, TB])
        hid_hi, hid_lo = (sb(n, [P, 2, TB], F32R) for n in ("hid_hi", "hid_lo"))
        ln_p = sb("ln_p", [P, SEQ, 3, V])
        z01 = sb("z01", [P, 2, V])
        bias = sb("bias", [P, NROW])
        bd_all = sb("bd_all", [P, B * MT])
        bd_cur = sb("bd_cur", [P, SEQ * MT])
        codes_i = sb("codes_i", [P, B], I32)
        codes_f = sb("codes_f", [P, B])
        feat_i = sb("feat_i", [P, KT], I32)
        feat_f = sb("feat_f", [P, KT])
        cb_all = sb("cb_all", [P, NB, KT, SEQ])
        cb_cur = sb("cb_cur", [P, KT, SEQ])
        exp_i = sb("exp_i", [1, B], I32)
        exp_n = sb("exp_n", [1, B])
        exp_f = sb("exp_f", [1, B])
        exp_id = sb("exp_id", [1, B], I32)
        mx = sb("mx", [P, TT])
        nmx = sb("nmx", [P, TT])
        rsum = sb("rsum", [P, TT])
        rinv = sb("rinv", [P, TT])
        stat = sb("stat", [P, TT, 6])
        mv = sb("mv", [P, TT, 2])
        veps = sb("veps", [P, TT])
        rstd = sb("rstd", [P, TT])
        mhalf = sb("mhalf", [P, 1])
        nmr = sb("nmr", [P, TT])
        warm = sb("warm", [P, 1])

        z23 = probs[:, :, :].rearrange("p (z a) t -> p z (a t)", z=2)
        z = [z01[:, 0, :], z01[:, 1, :], z23[:, 0, :], z23[:, 1, :]]
        bias_rows = gel[0:NROW, 0, 0:P]
        bd_rows = z01[0:MT, :, :].rearrange("p a n -> p (a n)")
        wp_raw = w1_raw[:, :, :, :].rearrange("p a k n -> p (a k n)").rearrange("p (k n) -> p k n", k=KT)
        wk_raw = e_raw[:, :, :].rearrange("p a n -> p (a n)").rearrange("p (k n) -> p k n", k=KT)
        ps = [ctx.enter_context(nc.psum_tensor(f"bank{i}", [P, 512], F32)) for i in range(8)]

        wq_in, wk_in, wv_in = ([sem(f"w{w}_in{t}") for t in range(KT)] for w in "qkv")
        wp_in = sem("wp_in")
        bias_in, codes_in, experts_in, bd_in = sem("bias_in"), sem("codes_in"), sem("experts_in"), sem("bd_in")
        x_in, e_in, proj_in, ln_in, proj_out = sem("x_in"), sem("e_in"), sem("proj_in"), sem("ln_in"), sem("proj_out")
        w1_in = [sem(f"w1_in{s}") for s in range(2)]
        w2_in = [sem(f"w2_in{s}") for s in range(2)]
        nmr_done, act_norm, last_step = sem("nmr_done"), sem("act_norm"), sem("last_step")
        z_last, stored_last = sem("z_last"), sem("stored_last")
        e1_in, z_free = sem("e1_in"), sem("z_free")
        stored = [sem(f"stored{t}") for t in range(TT)]
        bias_mm, tr_mm, fold_mm = sem("bias_mm"), sem("tr_mm"), sem("fold_mm")
        y_mm, v_mm, s_mm, down_mm, pT_mm, pv_mm, up_mm = (sem(n) for n in (
            "y_mm", "v_mm", "s_mm", "down_mm", "pT_mm", "pv_mm", "up_mm"))
        l1_mm, l2_mm = sem("l1_mm"), sem("l2_mm")
        tr_hi, fold_hi, y_hi, v_hi, pT_h, ao_hi, cms_hi, xp_h, e_hi, h3_h, w1_h, w2_h, gelu_done, exp_done, wp_h = (
            sem(n) for n in ("tr_hi", "fold_hi", "y_hi", "v_hi", "pT_h", "ao_hi", "cms_hi", "xp_h", "e_hi",
                             "h3_h", "w1_h", "w2_h", "gelu_done", "exp_done", "wp_h"))
        tr_lo, fold_lo, y_lo, v_lo, pT_l, ao_lo, cms_lo, xp_l, e_lo, h3_l, w1_l, w2_l, hid_l, wp_l = (
            sem(n) for n in ("tr_lo", "fold_lo", "y_lo", "v_lo", "pT_l", "ao_lo", "cms_lo", "xp_l", "e_lo",
                             "h3_l", "w1_l", "w2_l", "hid_l", "wp_l"))
        consts, iotas, bias_ready, ids_step, ids_ready, cb_step, cur_bias = (sem(n) for n in (
            "consts", "iotas", "bias_ready", "ids_step", "ids_ready", "cb_step", "cur_bias"))
        ident_ready, max_done, nmax_done, rinv_done, probs_done = (sem(n) for n in (
            "ident_ready", "max_done", "nmax_done", "rinv_done", "probs_done"))
        sum_done, clip_done, z_sum, ln_step, rstd_done, z_norm, z_scaled, resid_done = (sem(n) for n in (
            "sum_done", "clip_done", "z_sum", "ln_step", "rstd_done", "z_norm", "z_scaled", "resid_done"))
        L1_0, L2_0, HID_0, GELU_0, Z_0, Z_FREE_0 = 2, 2 * KT, 2, UNR, TT, 1

        def mm3(dst, w_hi, w_lo, a_hi, a_lo, start, stop, **kw):
            nc.tensor.matmul(dst, w_lo, a_hi, start=start, stop=False, **kw)
            nc.tensor.matmul(dst, w_hi, a_hi, start=False, stop=False, **kw)
            return nc.tensor.matmul(dst, w_hi, a_lo, start=False, stop=stop, **kw)

        def pe_transpose(src, bank0):
            for k in range(KT):
                for t in range(KT):
                    last = nc.tensor.transpose(ps[bank0 + k][:, t * P:(t + 1) * P],
                                               src[:, t, k * P:(k + 1) * P], ident[:, :])
                last.then_inc(tr_mm, 1)

        def pe_attention_1(pe, n, first):
            pe.wait_ge(x_in, 16 * (n + 1))
            if first:
                pe.wait_ge(fold_lo, KT)
            pe_transpose(x_raw, 4)
            if first:
                pe.wait_ge(fold_lo, 2 * KT)
            else:
                pe.wait_ge(proj_in, n * 64)
            for k in range(KT):
                pe.wait_ge(tr_lo, 12 + n * KT + k + 1)
                for j in range(KT):
                    if k == 0 and not first:
                        pe.wait_ge(sum_done, (n - 1) * KT + j + 1)
                    last = mm3(ps[j][:, :], aw_hi[:, 0, k * V + j * P:k * V + (j + 1) * P],
                               aw_lo[:, 0, k * V + j * P:k * V + (j + 1) * P],
                               x_hi[:, k, :], x_lo[:, k, :], k == 0, k == KT - 1)
                    if k == KT - 1:
                        last.then_inc(y_mm, 1)

            def values(tiles):
                for t in tiles:
                    for k in range(KT):
                        last = mm3(ps[4 + t][:, :], x_hi[:, k, t * P:(t + 1) * P], x_lo[:, k, t * P:(t + 1) * P],
                                   aw_hi[:, 1, k * V:(k + 1) * V], aw_lo[:, 1, k * V:(k + 1) * V],
                                   k == 0, k == KT - 1)
                    last.then_inc(v_mm, 1)

            values(range(TS) if first else range(TT))
            pe.wait_ge(y_lo, n * KT + KT)
            for t in range(TT):
                seq = slice(t // TS * T, (t // TS + 1) * T)
                for k in range(KT):
                    last = mm3(ps[t][:, 0:T], ya_hi[:, k, t * P:(t + 1) * P], ya_lo[:, k, t * P:(t + 1) * P],
                               x_hi[:, k, seq], x_lo[:, k, seq], k == 0, k == KT - 1)
                last.then_inc(s_mm, 1)
            if first:
                pe_bias_columns(pe)
                for b in range(SEQ):
                    values((TS + b,))
                    if b == 0:
                        pe.wait_ge(bias_ready, 2)
                    pe_probs_T(pe, 0, b, 4)

        def pe_bias_columns(pe):
            pe.wait_ge(v_lo, 1)
            pe.wait_ge(bias_in, 16 * len(BIAS))
            nc.tensor.transpose(ps[4][:, 0:NROW], bias_rows[0:NROW, :], ident[0:NROW, 0:NROW])
            pe.wait_ge(bd_in, 16 * B)
            for b in range(B):
                last = nc.tensor.transpose(ps[4][:, 64 + MT * b:64 + MT * (b + 1)],
                                           bd_rows[0:MT, b * P:(b + 1) * P], ident[0:MT, 0:MT])
            last.then_inc(bias_mm, 1)

        def pe_probs_T(pe, n, b, bank0):
            if b == 0 and bank0 == 6:
                pe.wait_ge(v_lo, n * TT + TT)
            pe.wait_ge(probs_done, n * TT + (b + 1) * TS)
            for u in range(TS):
                for s in range(TS):
                    last = nc.tensor.transpose(ps[bank0 + b][:, u * T + s * P:u * T + (s + 1) * P],
                                               probs[:, b * TS + s, u * P:(u + 1) * P], ident[:, :])
            last.then_inc(pT_mm, 1)

        def pe_attend(pe, n):
            for b in range(SEQ):
                pe.wait_ge(pT_l, n * SEQ + b + 1)
                pe.wait_ge(v_lo, n * TT + (b + 1) * TS)
                for e in range(KT):
                    for u in range(TS):
                        w = b * TS + u
                        last = mm3(ps[e][:, b * T:(b + 1) * T], vc_hi[:, w, e * P:(e + 1) * P],
                                   vc_lo[:, w, e * P:(e + 1) * P], pT_hi[:, b, u * T:(u + 1) * T],
                                   pT_lo[:, b, u * T:(u + 1) * T], u == 0, u == TS - 1)
                    if b == SEQ - 1:
                        last.then_inc(pv_mm, 1)

        def pe_down(pe, n, m, b):
            if m == 0:
                if b == 0:
                    pe.wait_ge(v_lo, n * TT + 2 * TT)
                pe.wait_ge(e_lo, n * SEQ + b + 1)
            for k in range(KT):
                if m == 0 and b == 0:
                    pe.wait_ge(xp_l, n * KT + k + 1)
                w = slice(k * BN + m * P, k * BN + (m + 1) * P)
                last = mm3(ps[4 + m][:, b * T:(b + 1) * T], aw_hi[:, b, w], aw_lo[:, b, w],
                           xp_hi[:, k, b * T:(b + 1) * T], xp_lo[:, k, b * T:(b + 1) * T], k == 0, k == KT - 1)
            if b == SEQ - 1:
                last.then_inc(down_mm, 1)

        def pe_down_last(pe):
            pe.wait_ge(e_lo, NB * SEQ)
            for k in range(KT):
                pe.wait_ge(xp_l, (NB - 1) * KT + k + 1)
                for i, (b, m) in enumerate(LAST_DOWN):
                    w = slice(k * BN + m * P, k * BN + (m + 1) * P)
                    last = mm3(ps[4 + i][:, 0:T], aw_hi[:, b, w], aw_lo[:, b, w], xp_hi[:, k, b * T:(b + 1) * T],
                               xp_lo[:, k, b * T:(b + 1) * T], k == 0, k == KT - 1)
                    if k == KT - 1:
                        last.then_inc(down_mm, 1)

        def pe_up(pe, n, bank0):
            def residual(t):
                for k in range(KT):
                    nc.tensor.matmul(ps[bank0 + t][:, k * P:(k + 1) * P], resid[:, k, t * P:(t + 1) * P], ident[:, :],
                                     start=k == 0, stop=True, skip_group_check=True)

            def product(t):
                b, tok = t // TS, slice(t * P, (t + 1) * P)
                for m in range(MT):
                    w = slice(KT * BN + m * V, KT * BN + (m + 1) * V)
                    last = mm3(ps[bank0 + t][:, :], h3_hi[:, m, tok], h3_lo[:, m, tok], aw_hi[:, b, w], aw_lo[:, b, w],
                               False, True, skip_group_check=True)
                last.then_inc(up_mm, 1)

            last = bank0 == 0
            for t in UP_ORDER[:2]:
                residual(t)
            pe.wait_ge(h3_l, n * MT + (SEQ if last else MT))
            for t in UP_ORDER[:2]:
                product(t)
            for t in UP_ORDER[2:]:
                residual(t)
                if last:
                    pe.wait_ge(h3_l, n * MT + 2 * SEQ)
                product(t)

        def pe_mlp(pe, n, phase):
            src = ((ya_hi, ya_lo, 0), (vc_hi, vc_lo, KT))

            def l1(q, g, part, first=False):
                a_hi, a_lo, k0 = src[part]
                for k in range(KT):
                    if part == 1:
                        pe.wait_ge(cms_lo, n * KT + k + 1)
                    elif first:
                        pe.wait_ge(ao_lo, n * KT + k + 1)
                    last = mm3(ps[4 + q][:, :], w1_hi[:, q % 2, k0 + k, :], w1_lo[:, q % 2, k0 + k, :],
                               a_hi[:, k, :], a_lo[:, k, :], k0 + k == 0, part == phase and k == KT - 1)
                if part == phase:
                    last.then_inc(l1_mm, 1)

            def begin(q, g, first=False):
                pe.wait_ge(w1_l, g + 1)
                pe.wait_ge(gelu_done, g - UNR + 1 + GELU_0)
                if phase == 0:
                    pe.wait_ge(z_sum, n * TT + UP_ORDER.index(q) + 1)
                l1(q, g, 0, first)

            def l2(q, g, c):
                pe.wait_ge(w2_l, g + 1)
                pe.wait_ge(hid_l, g + 1 + HID_0)
                for j in range(KT):
                    w = slice(j * P, (j + 1) * P)
                    mm3(ps[j][:, :], w2_hi[:, q % 2, w], w2_lo[:, q % 2, w], hid_hi[:, q % 2, :],
                        hid_lo[:, q % 2, :], c, True, skip_group_check=True).then_inc(l2_mm, 1)

            def turn(g0, first):
                g = [g0 + q for q in range(UNR)]
                begin(0, g[0], first and phase == 0)
                begin(1, g[1])
                if phase:
                    l1(0, g[0], 1)
                    l1(1, g[1], 1)
                l2(0, g[0], first)
                for q in range(2, UNR):
                    begin(q, g[q])
                    if phase:
                        l1(q, g[q], 1)
                    l2(q - 1, g[q - 1], False)
                l2(UNR - 1, g[UNR - 1], False)

            base = n * CH + phase * NCH
            turn(base, True)
            with pe.Fori(1, ITS) as it:
                turn(base + it * UNR, False)

        def pe_program(pe):
            pe.sem_inc(l1_mm, L1_0)
            pe.sem_inc(l2_mm, L2_0)
            pe.wait_ge(ident_ready, 1)
            for src, landed, bank0 in ((x_raw, wq_in, 0), (wk_raw, wk_in, KT), (resid, wv_in, 0)):
                if landed is wv_in:
                    pe.wait_ge(tr_lo, KT)
                for t in range(KT):
                    pe.wait_ge(landed[t], 16)
                    for k in range(KT):
                        last = nc.tensor.transpose(ps[bank0 + k][:, t * P:(t + 1) * P],
                                                   src[:, t, k * P:(k + 1) * P], ident[:, :])
                        if t == KT - 1:
                            last.then_inc(tr_mm, 1)
            for m in range(KT):
                for k in range(KT):
                    if m == 0:
                        pe.wait_ge(tr_lo, KT + k + 1)
                    last = mm3(ps[4 + m][:, :], ya_hi[:, k, m * P:(m + 1) * P], ya_lo[:, k, m * P:(m + 1) * P],
                               vc_hi[:, k, :], vc_lo[:, k, :], k == 0, k == KT - 1)
                last.then_inc(fold_mm, 1)
            pe.wait_ge(tr_lo, 3 * KT)
            pe.wait_ge(wp_l, 1)
            for m in range(KT):
                for k in range(KT):
                    last = mm3(ps[m][:, :], xp_hi[:, k, m * P:(m + 1) * P], xp_lo[:, k, m * P:(m + 1) * P],
                               x_hi[:, k, :], x_lo[:, k, :], k == 0, k == KT - 1)
                last.then_inc(fold_mm, 1)
            pe_attention_1(pe, 0, True)
            pe_attend(pe, 0)

            def mlps(n):
                pe_mlp(pe, n, 0)
                pe_mlp(pe, n, 1)

            with pe.Fori(0, NB - 1) as n:
                mlps(n)
                pe_attention_1(pe, n + 1, False)
                for m, b in ((0, 0), (0, 1), (1, 0), (1, 1)):
                    pe_down(pe, n, m, b)
                    if m:
                        pe_probs_T(pe, n + 1, b, 6)
                pe_attend(pe, n + 1)
                pe_up(pe, n, 4)
            mlps(NB - 1)
            pe_down_last(pe)
            pe_up(pe, NB - 1, 0)

        def slot_views(phase, s):
            k = KIN[phase]
            return w1_hi[:, s, 0:k, :], w1_lo[:, s, 0:k, :], w1_raw[:, s, 0:k, :]

        def act_w1(act, phase, q, g, pair):
            act.wait_ge(w1_in[q % 2], 16 * pair + 16)
            act.wait_ge(l1_mm, g - 2 + 1 + L1_0)
            hi, _, raw = slot_views(phase, q % 2)
            nc.scalar.activation(hi, raw, ACT.Copy).then_inc(w1_h, 1)

        def act_w2(act, q, g, pair):
            act.wait_ge(w2_in[q % 2], 16 * pair + 16)
            act.wait_ge(l2_mm, (g - 2 + 1) * KT + L2_0)
            nc.scalar.activation(w2_hi[:, q % 2, :], w2_raw[:, q % 2, :], ACT.Copy).then_inc(w2_h, 1)

        def act_gelu(act, phase, q, g, col):
            act.wait_ge(l1_mm, g + 1 + L1_0)
            act.wait_ge(l2_mm, (g - 2 + 1) * KT + L2_0)
            act.wait_ge(hid_l, g - 2 + 1 + HID_0)
            b = bias[:, bass.ds(MLP_B[phase] + col, 1)] if not isinstance(col, int) else \
                bias[:, MLP_B[phase] + col:MLP_B[phase] + col + 1]
            nc.scalar.activation(hid_hi[:, q % 2, :], ps[4 + q][:, :], ACT.Gelu, bias=b)
            nc.scalar.activation(gel[:, q % 2, :], ps[4 + q][:, :], ACT.Gelu, bias=b).then_inc(gelu_done, 1)

        def chunk_steps(phase, n, it, last, w1, w2, gelu):
            q0 = phase * NCH
            g0 = n * CH + q0 + it * UNR
            h0 = n * NCH + (q0 + it * UNR) // 2 if isinstance(it, int) else n * NCH + q0 // 2 + it * (UNR // 2)
            nxt = 1 if last and phase == 0 else (0 if last else phase)
            w1n = lambda q: w1(nxt if q >= UNR else phase, q % UNR, g0 + q, h0 + q // 2)
            w2n = lambda q: w2(q % UNR, g0 + q, h0 + q // 2)
            more = not (last and phase == 1 and isinstance(n, int))
            col = it * UNR
            gelu(phase, 0, g0, col)
            w1n(2)
            gelu(phase, 1, g0 + 1, col + 1)
            w1n(3)
            w2n(2)
            gelu(phase, 2, g0 + 2, col + 2)
            w2n(3)
            if more:
                w1n(4)
            gelu(phase, 3, g0 + 3, col + 3)
            if more:
                w2n(4)
                w1n(5)
                if not last:
                    w2n(5)

        def act_tiles(act, mm, n0, banks, hi, sem_out, func=ACT.Copy, tiles=range(4), **kw):
            for k in tiles:
                bank = banks[k]
                act.wait_ge(mm, n0 + k + 1)
                nc.scalar.activation(hi[:, k, :], ps[bank][:, :], func,
                                     **{a: f(k) for a, f in kw.items()}).then_inc(sem_out, 1)

        def act_attention_1(act, n, first):
            if not first:
                act.wait_ge(resid_done, n * 3)
            act_tiles(act, tr_mm, 12 + n * KT, range(4, 8), x_hi, tr_hi)
            act_tiles(act, y_mm, n * KT, range(4), ya_hi, y_hi)

        def act_values(act, n, tiles=range(4)):
            act_tiles(act, v_mm, n * KT, range(4, 8), vc_hi, v_hi, tiles=tiles)

        def act_exps(act, n):
            if not isinstance(n, int):
                act.wait_ge(z_free, n)
            for t in range(TT):
                act.wait_ge(nmax_done, n * TT + t + 1)
                nc.scalar.activation(probs[:, t, :], ps[t][:, 0:T], ACT.Exp, bias=nmx[:, t:t + 1], scale=SCALE,
                                     accum_out=rsum[:, t:t + 1]).then_inc(exp_done, 1)

        def act_probs_T(act, n, bank0, seqs=range(SEQ)):
            for b in seqs:
                act.wait_ge(pT_mm, n * SEQ + b + 1)
                nc.scalar.activation(pT_hi[:, b, :], ps[bank0 + b][:, :], ACT.Copy).then_inc(pT_h, 1)

        def act_attention(act, n):
            act_tiles(act, pv_mm, n * KT, range(4), ya_hi, ao_hi, ACT.Identity,
                      bias=lambda k: bias[:, BP + k:BP + k + 1])

        def act_expert_weights(act, n, b):
            act.wait_ge((e_in, e1_in)[b], 32 * n + 32)
            nc.scalar.activation(aw_hi[:, b, :], e_raw[:, :, :].rearrange("p a n -> p (a n)"), ACT.Copy)\
                .then_inc(e_hi, 1)

        def act_down(act, n):
            for m in range(MT):
                act.wait_ge(down_mm, n * MT + m + 1)
                for b in range(SEQ):
                    col, cols = bd_cur[:, b * MT + m:b * MT + m + 1], slice(b * T, (b + 1) * T)
                    nc.scalar.activation(h3_hi[:, m, cols], ps[4 + m][:, cols], ACT.Gelu, bias=col)
                    last = nc.scalar.activation(gel[:, m, cols], ps[4 + m][:, cols], ACT.Gelu, bias=col)
                last.then_inc(h3_h, 1)

        def act_down_last(act):
            for i, (b, m) in enumerate(LAST_DOWN):
                act.wait_ge(down_mm, (NB - 1) * MT + i + 1)
                col, cols = bd_cur[:, b * MT + m:b * MT + m + 1], slice(b * T, (b + 1) * T)
                nc.scalar.activation(h3_hi[:, m, cols], ps[4 + i][:, 0:T], ACT.Gelu, bias=col)
                nc.scalar.activation(gel[:, m, cols], ps[4 + i][:, 0:T], ACT.Gelu, bias=col).then_inc(h3_h, 1)

        def act_xp(act, n):
            for j in range(KT):
                act.wait_ge(clip_done, n * KT + j + 1)
                nc.scalar.activation(xp_hi[:, j, :], resid[:, j, :], ACT.Copy).then_inc(xp_h, 1)

        def act_norm_last(act):
            for i, t in enumerate(UP_ORDER[:TS]):
                act.wait_ge(nmr_done, i + 1)
                nc.scalar.activation(z[t], z[t], ACT.Identity, bias=nmr[:, t:t + 1], scale=rstd[:, t:t + 1])\
                    .then_inc(act_norm, 1)

        def act_program(act):
            act.sem_inc(gelu_done, GELU_0)
            act.dma_start(exp_i[:, :], row_of(experts)).then_inc(experts_in, 16)
            act_tiles(act, tr_mm, 0, range(4), ya_hi, tr_hi)
            for (src, n), off in zip(BIAS, offs):
                act.dma_start(bias_rows[off:off + n // P, :], src.rearrange("(r p) -> r p", p=P)).then_inc(bias_in, 16)
            act_tiles(act, tr_mm, KT, range(4, 8), vc_hi, tr_hi)
            act_tiles(act, tr_mm, 2 * KT, range(4), xp_hi, tr_hi)
            act.wait_ge(wp_in, 16)
            nc.scalar.activation(x_hi[:, :, :], wp_raw, ACT.Copy).then_inc(wp_h, 1)
            for slot, banks in ((0, range(4, 8)), (1, range(4))):
                for m, bank in enumerate(banks):
                    act.wait_ge(fold_mm, slot * KT + m + 1)
                    nc.scalar.activation(aw_hi[:, slot, m * V:(m + 1) * V], ps[bank][:, :], ACT.Copy)\
                        .then_inc(fold_hi, 1)
            act_attention_1(act, 0, True)
            act_w1(act, 0, 0, 0, 0)
            act_w2(act, 0, 0, 0)
            act_values(act, 0, range(TS))
            act_w1(act, 0, 1, 1, 0)
            act_w2(act, 1, 1, 0)
            act_exps(act, 0)
            for b in range(SEQ):
                act_values(act, 0, (TS + b,))
                act_probs_T(act, 0, 4, (b,))
            act.wait_ge(bias_ready, 2)
            nc.scalar.activation(warm[:, :], bias[:, 0:1], ACT.Gelu)
            act_attention(act, 0)

            def mlps(n):
                for phase in range(2):
                    steps = lambda it, last: chunk_steps(
                        phase, n, it, last, lambda ph, q, g, h: act_w1(act, ph, q, g, h),
                        lambda q, g, h: act_w2(act, q, g, h), lambda ph, q, g, c: act_gelu(act, ph, q, g, c))
                    if phase == 1 and isinstance(n, int):
                        with act.Fori(0, ITS - 2) as it:
                            steps(it, False)
                        act_expert_weights(act, n, 0)
                        steps(ITS - 2, False)
                        act_expert_weights(act, n, 1)
                    else:
                        with act.Fori(0, ITS - 1) as it:
                            steps(it, False)
                    steps(ITS - 1, True)
                    if phase == 0:
                        act.wait_ge(cur_bias, n * 2 + 2)
                        for j in range(KT):
                            act.wait_ge(l2_mm, (n * CH + NCH - 1) * KT + j + 1 + L2_0)
                            for b in range(SEQ):
                                cols = slice(b * T, (b + 1) * T)
                                last = nc.scalar.activation(vc_hi[:, j, cols], ps[j][:, cols], ACT.Identity,
                                                            bias=cb_cur[:, j, b:b + 1])
                            last.then_inc(cms_hi, 1)
                        act_w2(act, 1, n * CH + NCH + 1, n * NCH + NCH // 2)

            with act.Fori(0, NB - 1) as n:
                mlps(n)
                act_attention_1(act, n + 1, False)
                act_w2(act, 1, n * CH + CH + 1, n * NCH + NCH)
                act_expert_weights(act, n, 0)
                act_xp(act, n)
                act_values(act, n + 1)
                act_expert_weights(act, n, 1)
                nc.scalar.activation(warm[:, :], bias[:, 0:1], ACT.Exp)
                act_exps(act, n + 1)
                act_probs_T(act, n + 1, 6)
                act_down(act, n)
                act_attention(act, n + 1)
            mlps(NB - 1)
            act_xp(act, NB - 1)
            act_down_last(act)
            act_norm_last(act)

        sub = lambda dst, a, hi: nc.vector.tensor_tensor(dst, a, hi.bitcast(F32), ALU.subtract)

        def dve_w1(dve, phase, q, g, pair):
            dve.wait_ge(w1_h, g + 1)
            hi, lo, raw = slot_views(phase, q % 2)
            sub(lo, raw, hi).then_inc(w1_l, 1)

        def dve_w2(dve, q, g, pair):
            dve.wait_ge(w2_h, g + 1)
            sub(w2_lo[:, q % 2, :], w2_raw[:, q % 2, :], w2_hi[:, q % 2, :]).then_inc(w2_l, 1)

        def dve_gelu(dve, phase, q, g, col):
            dve.wait_ge(gelu_done, g + 1 + GELU_0)
            sub(hid_lo[:, q % 2, :], gel[:, q % 2, :], hid_hi[:, q % 2, :]).then_inc(hid_l, 1)

        def dve_tiles(dve, hi_sem, n0, banks, hi, lo, lo_sem, tiles=range(4)):
            for k in tiles:
                bank = banks[k]
                dve.wait_ge(hi_sem, n0 + k + 1)
                sub(lo[:, k, :], ps[bank][:, :], hi[:, k, :]).then_inc(lo_sem, 1)

        def dve_y(dve, n):
            dve_tiles(dve, y_hi, n * KT, range(4), ya_hi, ya_lo, y_lo)

        def dve_v(dve, n, tiles=range(4)):
            dve_tiles(dve, v_hi, n * KT, range(4, 8), vc_hi, vc_lo, v_lo, tiles)

        def dve_softmax(dve, n):
            def row_max(t):
                dve.wait_ge(s_mm, n * TT + t + 1)
                nc.vector.reduce_max(mx[:, t:t + 1], ps[t][:, 0:T], AX_X).then_inc(max_done, 1)

            def shift(t):
                dve.wait_ge(max_done, n * TT + t + 1)
                nc.vector.tensor_scalar_mul(nmx[:, t:t + 1], mx[:, t:t + 1], -SCALE).then_inc(nmax_done, 1)

            row_max(0)
            for t in range(1, TT):
                row_max(t)
                shift(t - 1)
            shift(TT - 1)

        def dve_probs(dve, n):
            for t in range(TT):
                dve.wait_ge(exp_done, n * TT + t + 1)
                nc.vector.reciprocal(rinv[:, t:t + 1], rsum[:, t:t + 1]).then_inc(rinv_done, 1)
                dve.wait_ge(rinv_done, n * TT + t + 1)
                nc.vector.tensor_scalar_mul(probs[:, t, :], probs[:, t, :], rinv[:, t:t + 1])\
                    .then_inc(probs_done, 1)

        def dve_probs_T(dve, n, bank0, seqs=range(SEQ)):
            for b in seqs:
                dve.wait_ge(pT_h, n * SEQ + b + 1)
                sub(pT_lo[:, b, :], ps[bank0 + b][:, :], pT_hi[:, b, :]).then_inc(pT_l, 1)

        def dve_attention(dve, n):
            for e in range(KT):
                dve.wait_ge(ao_hi, n * KT + e + 1)
                nc.vector.scalar_tensor_tensor(out=ya_lo[:, e, :], in0=ps[e][:, :], scalar=bias[:, BP + e:BP + e + 1],
                                               in1=ya_hi[:, e, :].bitcast(F32), op0=ALU.add, op1=ALU.subtract)\
                    .then_inc(ao_lo, 1)

        def dve_expert_weights(dve, n, b):
            dve.wait_ge(e_hi, n * SEQ + b + 1)
            sub(aw_lo[:, b, :], e_raw[:, :, :].rearrange("p a n -> p (a n)"), aw_hi[:, b, :]).then_inc(e_lo, 1)

        def dve_sum(dve, n, j):
            if j == 0:
                dve.wait_ge(resid_done, n * 3 + 3)
            dve.wait_ge(l2_mm, (n * CH + CH - 1) * KT + j + 1 + L2_0)
            nc.vector.scalar_tensor_tensor(out=resid[:, j, :], in0=ps[j][:, :], scalar=bias[:, MB2 + j:MB2 + j + 1],
                                           in1=resid[:, j, :], op0=ALU.add, op1=ALU.add).then_inc(sum_done, 1)

        def dve_clip(dve, n, j):
            dve.wait_ge(sum_done, n * KT + j + 1)
            nc.vector.tensor_scalar(resid[:, j, :], resid[:, j, :], 0.0, 1.0, ALU.max, ALU.min).then_inc(clip_done, 1)

        def dve_xp(dve, n, j):
            dve.wait_ge(xp_h, n * KT + j + 1)
            sub(xp_lo[:, j, :], resid[:, j, :], xp_hi[:, j, :]).then_inc(xp_l, 1)

        def dve_x_lo(dve, n, k):
            dve.wait_ge(tr_hi, 12 + n * KT + k + 1)
            sub(x_lo[:, k, :], ps[4 + k][:, :], x_hi[:, k, :]).then_inc(tr_lo, 1)

        def dve_h3(dve, n):
            for m in range(MT):
                dve.wait_ge(h3_h, n * MT + m + 1)
                sub(h3_lo[:, m, :], gel[:, m, :], h3_hi[:, m, :]).then_inc(h3_l, 1)

        def dve_h3_last(dve):
            for i, (b, m) in enumerate(LAST_DOWN):
                cols = slice(b * T, (b + 1) * T)
                dve.wait_ge(h3_h, (NB - 1) * MT + i + 1)
                sub(h3_lo[:, m, cols], gel[:, m, cols], h3_hi[:, m, cols]).then_inc(h3_l, 1)

        def dve_layer_norm(dve, n, last):
            def stats(i):
                t = UP_ORDER[i]
                dve.wait_ge(up_mm, n * TT + i + 1)
                if i == 0:
                    dve.wait_ge(ln_in, 16 * 3 * SEQ * (n + 1))
                    dve.wait_ge(z_free, n + Z_FREE_0)
                nc.vector.tensor_tensor(z[t], ps[t if last else 4 + t][:, :], ln_p[:, t // TS, 0, :], ALU.add)\
                    .then_inc(z_sum, 1)
                dve.wait_ge(z_sum, n * TT + i + 1 + Z_0)
                nc.vector.bn_stats(stat[:, t, :], z[t]).then_inc(ln_step, 1)
                dve.drain()
                nc.vector.bn_aggr(mv[:, t, :], stat[:, t, :]).then_inc(ln_step, 1)
                dve.wait_ge(ln_step, n * 3 * TT + 3 * i + 2)
                nc.vector.tensor_scalar_add(veps[:, t:t + 1], mv[:, t, 1:2], LN_EPS).then_inc(ln_step, 1)

            def norm(i):
                t = UP_ORDER[i]
                dve.wait_ge(rstd_done, n * TT + i + 1)
                if last:
                    nc.vector.scalar_tensor_tensor(out=nmr[:, t:t + 1], in0=mv[:, t, 0:1], scalar=-1.0,
                                                   in1=rstd[:, t:t + 1], op0=ALU.mult, op1=ALU.mult)\
                        .then_inc(nmr_done, 1)
                else:
                    nc.vector.tensor_scalar(z[t], z[t], mv[:, t, 0:1], rstd[:, t:t + 1], ALU.subtract, ALU.mult)\
                        .then_inc(z_norm, 1)

            stats(0)
            for i in range(1, TT):
                stats(i)
                if not last or i <= TS:
                    norm(i - 1)
            if not last:
                norm(TT - 1)
                return
            for i in range(TS, TT):
                t = UP_ORDER[i]
                nc.vector.scalar_tensor_tensor(out=z[t], in0=z[t], scalar=mv[:, t, 0:1], in1=ln_p[:, t // TS, 1, :],
                                               op0=ALU.subtract, op1=ALU.mult).then_inc(last_step, 1)
            for i in range(TS, TT):
                t = UP_ORDER[i]
                dve.wait_ge(rstd_done, n * TT + i + 1)
                dve.wait_ge(last_step, i - TS + 1)
                nc.vector.scalar_tensor_tensor(out=z[t], in0=z[t], scalar=rstd[:, t:t + 1], in1=ln_p[:, t // TS, 2, :],
                                               op0=ALU.mult, op1=ALU.add).then_inc(z_last, 1)

        def dve_columns(n):
            nc.vector.tensor_copy(bd_cur[:, :], bd_all[:, bass.ds(n * (SEQ * MT), SEQ * MT)]).then_inc(cur_bias, 1)
            flat = cb_all[:, :, :, :].rearrange("p n k s -> p (n k s)")
            nc.vector.tensor_copy(cb_cur[:, :, :].rearrange("p k s -> p (k s)"),
                                  flat[:, bass.ds(n * (KT * SEQ), KT * SEQ)]).then_inc(cur_bias, 1)

        def dve_program(dve):
            dve.sem_inc(hid_l, HID_0)
            dve.sem_inc(z_sum, Z_0)
            nc.vector.memset(mhalf[:, :], -0.5).then_inc(consts, 1)
            dve.wait_ge(experts_in, 16)
            nc.vector.tensor_scalar(exp_n[:, :], exp_i[:, :], 0.0, float(E), ALU.is_lt, ALU.mult).then_inc(ids_step, 1)
            dve.wait_ge(ids_step, 1)
            nc.vector.tensor_tensor(exp_f[:, :], exp_n[:, :], exp_i[:, :], ALU.add).then_inc(ids_step, 1)
            dve.wait_ge(ids_step, 2)
            nc.vector.tensor_scalar(exp_id[:, :], exp_f[:, :], 0.0, float(E - 1), ALU.max, ALU.min)\
                .then_inc(ids_ready, 1)
            dve.wait_ge(ident_ready, 1)
            dve_tiles(dve, tr_hi, 0, range(4), ya_hi, ya_lo, tr_lo)
            dve_tiles(dve, tr_hi, KT, range(4, 8), vc_hi, vc_lo, tr_lo)
            dve_tiles(dve, tr_hi, 2 * KT, range(4), xp_hi, xp_lo, tr_lo)
            dve.wait_ge(wp_h, 1)
            sub(x_lo[:, :, :], wp_raw, x_hi[:, :, :]).then_inc(wp_l, 1)
            for slot, banks in ((0, range(4, 8)), (1, range(4))):
                for m, bank in enumerate(banks):
                    dve.wait_ge(fold_hi, slot * KT + m + 1)
                    cols = slice(m * V, (m + 1) * V)
                    sub(aw_lo[:, slot, cols], ps[bank][:, :], aw_hi[:, slot, cols]).then_inc(fold_lo, 1)
            for k in range(KT):
                dve_x_lo(dve, 0, k)
            dve_y(dve, 0)
            dve_w1(dve, 0, 0, 0, 0)
            dve_w2(dve, 0, 0, 0)
            dve_v(dve, 0, range(TS))
            dve_w1(dve, 0, 1, 1, 0)
            dve_w2(dve, 1, 1, 0)
            dve_softmax(dve, 0)
            dve_probs(dve, 0)
            dve.wait_ge(bias_mm, 1)
            nc.vector.tensor_copy(bias[:, :], ps[4][:, 0:NROW]).then_inc(bias_ready, 1)
            nc.vector.tensor_copy(bd_all[:, :], ps[4][:, 64:64 + B * MT]).then_inc(bias_ready, 1)
            dve.wait_ge(codes_in, 16)
            dve.wait_ge(iotas, 1)
            nc.vector.tensor_copy(codes_f[:, :], codes_i[:, :]).then_inc(cb_step, 1)
            nc.vector.tensor_copy(feat_f[:, :], feat_i[:, :]).then_inc(cb_step, 1)
            dve.wait_ge(cb_step, 2)
            dve.wait_ge(bias_ready, 2)
            for k in range(KT):
                nc.vector.tensor_scalar(cb_all[:, :, k, :], codes_f[:, :].rearrange("p (n s) -> p n s", s=SEQ),
                                        feat_f[:, k:k + 1], bias[:, CB2 + k:CB2 + k + 1], ALU.is_equal, ALU.add)\
                    .then_inc(cb_step, 1)
            dve.wait_ge(cb_step, 2 + KT)
            for b in range(SEQ):
                dve_v(dve, 0, (TS + b,))
                dve_probs_T(dve, 0, 4, (b,))
            dve_attention(dve, 0)

            def mlps(n):
                dve_columns(n)
                for phase in range(2):
                    steps = lambda it, last: chunk_steps(
                        phase, n, it, last, lambda ph, q, g, h: dve_w1(dve, ph, q, g, h),
                        lambda q, g, h: dve_w2(dve, q, g, h), lambda ph, q, g, c: dve_gelu(dve, ph, q, g, c))
                    if phase == 1 and isinstance(n, int):
                        with dve.Fori(0, ITS - 2) as it:
                            steps(it, False)
                        dve_expert_weights(dve, n, 0)
                        steps(ITS - 2, False)
                        dve_expert_weights(dve, n, 1)
                    else:
                        with dve.Fori(0, ITS - 1) as it:
                            steps(it, False)
                    steps(ITS - 1, True)
                    if phase == 0:
                        dve.wait_ge(cur_bias, n * 2 + 2)
                        for j in range(KT):
                            dve.wait_ge(cms_hi, n * KT + j + 1)
                            for b in range(SEQ):
                                cols = slice(b * T, (b + 1) * T)
                                last = nc.vector.scalar_tensor_tensor(
                                    out=vc_lo[:, j, cols], in0=ps[j][:, cols], scalar=cb_cur[:, j, b:b + 1],
                                    in1=vc_hi[:, j, cols].bitcast(F32), op0=ALU.add, op1=ALU.subtract)
                            last.then_inc(cms_lo, 1)
                        dve_w2(dve, 1, n * CH + NCH + 1, 0)

            with dve.Fori(0, NB - 1) as n:
                mlps(n)
                dve_sum(dve, n, 0)
                for j in range(1, KT):
                    dve_sum(dve, n, j)
                    dve_x_lo(dve, n + 1, j - 1)
                dve_x_lo(dve, n + 1, KT - 1)
                for j in range(KT):
                    dve_clip(dve, n, j)
                dve_y(dve, n + 1)
                dve_w2(dve, 1, n * CH + CH + 1, 0)
                dve_expert_weights(dve, n, 0)
                for j in range(KT):
                    dve_xp(dve, n, j)
                dve_v(dve, n + 1)
                dve_expert_weights(dve, n, 1)
                dve_softmax(dve, n + 1)
                dve_probs(dve, n + 1)
                dve_probs_T(dve, n + 1, 6)
                dve_h3(dve, n)
                dve_attention(dve, n + 1)
                dve_layer_norm(dve, n, False)
            mlps(NB - 1)
            for j in range(KT):
                dve_sum(dve, NB - 1, j)
                dve_clip(dve, NB - 1, j)
                if j:
                    dve_xp(dve, NB - 1, j - 1)
            dve_xp(dve, NB - 1, KT - 1)
            dve_h3_last(dve)
            dve_layer_norm(dve, NB - 1, True)

        def pool_residual(pool, n):
            pool.wait_ge(cms_lo, n * KT + KT)
            nc.gpsimd.tensor_tensor(resid[:, :, :], vc_hi[:, :, :].bitcast(F32), vc_lo[:, :, :].bitcast(F32),
                                    ALU.add).then_inc(resid_done, 1)
            pool.wait_ge(resid_done, n * 3 + 1)
            nc.gpsimd.tensor_tensor(resid[:, :, :], resid[:, :, :], x_hi[:, :, :].bitcast(F32), ALU.add)\
                .then_inc(resid_done, 1)
            pool.wait_ge(resid_done, n * 3 + 2)
            nc.gpsimd.tensor_tensor(resid[:, :, :], resid[:, :, :], x_lo[:, :, :].bitcast(F32), ALU.add)\
                .then_inc(resid_done, 1)

        def load_expert(eng, n, b, landed):
            e = eng.value_load(exp_id[0:1, bass.ds(n * SEQ + b, 1)], min_val=0, max_val=E - 1)
            eng.dma_start(e_raw[:, 0, :].rearrange("p (k n) -> p k n", k=KT),
                          down_v[:, bass.ds(e * KT, KT), :]).then_inc(landed, 16)
            eng.dma_start(e_raw[:, 1, :].rearrange("p (k n) -> p k n", k=MT),
                          up_v[:, bass.ds(e * MT, MT), :]).then_inc(landed, 16)

        def pool_expert(pool, n, last):
            pool.wait_ge(e_lo, n * SEQ + 1)
            load_expert(pool, n, 1, e1_in)

            def power(i):
                t = UP_ORDER[i]
                pool.wait_ge(ln_step, n * 3 * TT + 3 * i + 3)
                nc.gpsimd.tensor_tensor(rstd[:, t:t + 1], veps[:, t:t + 1], mhalf[:, :], ALU.pow)\
                    .then_inc(rstd_done, 1)

            def scale(i):
                t = UP_ORDER[i]
                if last:
                    pool.wait_ge(act_norm, i + 1)
                else:
                    pool.wait_ge(z_norm, n * TT + i + 1)
                nc.gpsimd.tensor_tensor(z[t], z[t], ln_p[:, t // TS, 1, :], ALU.mult).then_inc(z_scaled, 1)

            def shift(i):
                t = UP_ORDER[i]
                pool.wait_ge(z_scaled, n * 2 * TT + 2 * i + 1)
                nc.gpsimd.tensor_tensor(z[t], z[t], ln_p[:, t // TS, 2, :], ALU.add).then_inc(z_scaled, 1)

            if last:
                power(0)
                power(1)
                scale(0)
                power(2)
                shift(0)
                power(3)
                scale(1)
                shift(1)
                return
            for i in range(TT):
                power(i)
            for i, t in enumerate(UP_ORDER):
                scale(i)
                shift(i)
                pool.wait_ge(z_scaled, n * 2 * TT + 2 * i + 2)
                pool.dma_start(out_rows[bass.ds(n * TB + t * P, P), :], z[t]).then_inc(stored[t], 16)
            for t in range(TT):
                pool.wait_ge(stored[t], 16 * n + 16)
            pool.sem_inc(z_free, 1)

        def pool_program(pool):
            pool.sem_inc(z_free, Z_FREE_0)
            nc.gpsimd.memset(ident[:, :], 0.0).then_inc(iotas, 1)
            nc.gpsimd.iota(feat_i[:, :], pattern=[[P, KT]], base=0, channel_multiplier=1).then_inc(iotas, 1)
            pool.wait_ge(iotas, 2)
            nc.gpsimd.affine_select(out=ident[:, :], in_=ident[:, :], compare_op=ALU.not_equal, fill=1.0, base=0,
                                    pattern=[[-1, P]], channel_multiplier=1).then_inc(ident_ready, 1)
            pool.wait_ge(ids_ready, 1)
            with pool.Fori(0, B) as b:
                e = pool.value_load(exp_id[0:1, bass.ds(b, 1)], min_val=0, max_val=E - 1)
                pool.dma_start(bd_rows[:, bass.ds(b * P, P)], bdown_v[bass.ds(e * MT, MT), :]).then_inc(bd_in, 16)
            pool.wait_ge(consts, 1)
            with pool.Fori(0, NB - 1) as n:
                pool_residual(pool, n)
                pool_expert(pool, n, False)
            pool_residual(pool, NB - 1)
            pool_expert(pool, NB - 1, True)

        def load_chunk(sp, phase, s, g, c):
            k = KIN[phase]
            sp.dma_start(w1_raw[:, s, 0:k, :], mlp_w1[phase][:, :, bass.ds(c, P)]).then_inc(w1_in[s], 16)
            sp.dma_start(w2_raw[:, s, :], mlp_w2[phase][bass.ds(c, P), :]).then_inc(w2_in[s], 16)

        def turn_loads(sp, n, more):
            def tokens():
                sp.wait_ge(tr_mm, 12 + n * KT + KT)
                sp.dma_start(x_raw[:, :, :], x_rows[bass.ds((n + 1) * TB, TB), :]
                             .rearrange("(t p) v -> p t v", p=P)).then_inc(x_in, 16)

            def projection(slot):
                sp.wait_ge(v_mm, n * TT + TT)
                sp.dma_start(aw_hi[:, slot, :].bitcast(F32), proj_hi[:, slot, :]).then_inc(proj_in, 16)
                sp.dma_start(aw_lo[:, slot, :].bitcast(F32), proj_lo[:, slot, :]).then_inc(proj_in, 16)

            def norm_rows(b):
                e = sp.value_load(exp_id[0:1, bass.ds(n * SEQ + b, 1)], min_val=0, max_val=E - 1)
                for i, src in enumerate(ln_v):
                    sp.dma_start(ln_p[:, b, i, :], src[bass.ds(e, 1), :].to_broadcast([P, V])).then_inc(ln_in, 16)

            own = [lambda: load_expert(sp, n, 0, e_in), lambda: norm_rows(0), lambda: norm_rows(1)]
            return own + [tokens, lambda: projection(0), lambda: projection(1)] if more else own

        def sync_program(sp):
            for dst, src, landed in zip((x_raw, wk_raw, resid), square, (wq_in, wk_in, wv_in)):
                for t in range(KT):
                    sp.dma_start(dst[:, t, :], src[:, t, :]).then_inc(landed[t], 16)
            sp.dma_start(codes_i[:, :], row_of(codes).to_broadcast([P, B])).then_inc(codes_in, 16)
            sp.dma_start(wp_raw, square[3]).then_inc(wp_in, 16)
            sp.wait_ge(tr_mm, KT)
            sp.dma_start(x_raw[:, :, :], x_rows[0:TB, :].rearrange("(t p) v -> p t v", p=P)).then_inc(x_in, 16)
            sp.wait_ge(wp_l, 1)
            load_chunk(sp, 0, 0, 0, 0)
            load_chunk(sp, 0, 1, 1, P)
            sp.wait_ge(fold_lo, 2 * KT)
            for slot in range(2):
                sp.dma_start(proj_hi[:, slot, :], aw_hi[:, slot, :].bitcast(F32)).then_inc(proj_out, 16)
                sp.dma_start(proj_lo[:, slot, :], aw_lo[:, slot, :].bitcast(F32)).then_inc(proj_out, 16)
            sp.wait_ge(ids_ready, 1)
            sp.wait_ge(proj_out, 64)

            def chunk_pair(phase, g, c):
                for s in range(2):
                    sp.wait_ge(w1_l, g + s - 1)
                    sp.wait_ge(w2_l, g + s - 1)
                    load_chunk(sp, phase, s, g + s, c + s * P)

            def mlps(n, more):
                with sp.Fori(1, NCH // 2) as j:
                    chunk_pair(0, n * CH + j * 2, j * (2 * P))
                sp.wait_ge(z_free, n + Z_FREE_0)
                pieces = turn_loads(sp, n, more)
                for j in range(NCH // 2):
                    chunk_pair(1, n * CH + NCH + j * 2, j * (2 * P))
                    if j < len(pieces):
                        pieces[j]()
                if more:
                    chunk_pair(0, n * CH + CH, 0)

            with sp.Fori(0, NB - 1) as n:
                mlps(n, True)
            mlps(NB - 1, False)
            for i in (0, 2, 3, 1):
                t = UP_ORDER[i]
                if i < TS:
                    sp.wait_ge(z_scaled, (NB - 1) * 2 * TT + 2 * i + 2)
                else:
                    sp.wait_ge(z_last, i - TS + 1)
                sp.dma_start(out_rows[(NB - 1) * TB + t * P:(NB - 1) * TB + (t + 1) * P, :], z[t])\
                    .then_inc(stored_last, 16)
            sp.wait_ge(stored_last, 16 * TT)

        block = ctx.enter_context(nc.Block())

        @block.sync
        def _(sp):
            sync_program(sp)

        @block.gpsimd
        def _(pool):
            pool_program(pool)

        @block.scalar
        def _(act):
            act_program(act)

        @block.vector
        def _(dve):
            dve_program(dve)

        @block.tensor
        def _(pe):
            pe_program(pe)


_INS = ['x', 'itok_B_17_1546', 'itok_B_1_2', 'L0_cond_Wq', 'L0_cond_Wk', 'L0_cond_Wv', 'L0_cond_Wp', 'L0_cond_bp',
        'L0_cond_cW1', 'L0_cond_cb1', 'L0_cond_cW2', 'L0_cond_cb2', 'L0_cond_mW1', 'L0_cond_mb1', 'L0_cond_mW2',
        'L0_cond_mb2', 'L1_cond_W_down', 'L1_cond_b_down', 'L1_cond_W_up', 'L1_cond_b_up', 'L1_cond_ln_w',
        'L1_cond_ln_b']


def kernel(**inputs):
    import numpy as np
    import concourse.bacc as bacc
    from concourse.bass_utils import run_bass_kernel_spmd as run

    nc = bacc.Bacc("TRN2", target_bir_lowering=False, num_devices=1)
    arrays, args = {}, []
    for name in _INS:
        a = np.ascontiguousarray(inputs[name])
        arrays[f"in_{name}"] = a
        args.append(nc.dram_tensor(f"in_{name}", a.shape, mybir.dt.from_np(a.dtype), kind="ExternalInput").ap())
    shape = inputs['x'].shape
    args.append(nc.dram_tensor("out_0", shape, F32, kind="ExternalOutput").ap())
    build(nc, *args)
    r = run(nc, [arrays], core_ids=[0])
    return r.results[0]["out_0"]
```
